# Optimizing a Trainium2 kernel written in Bass

```python
import numpy as np
import jax
import jax.numpy as jnp

def _softmax(x, axis=-1):
    return jax.nn.softmax(x, axis=axis)

def _gelu(x):
    return jax.nn.gelu(x, approximate=True)

def _silu(x):
    return jax.nn.silu(x)

def _sigmoid(x):
    return jax.nn.sigmoid(x)

def _layernorm(x, axis=-1, eps=1e-05):
    m = jnp.mean(x, axis=axis, keepdims=True)
    v = jnp.var(x, axis=axis, keepdims=True)
    return (x - m) / jnp.sqrt(v + eps)

def _scatter_add(tgt, idx, src, axis=0):
    return tgt.at[idx].add(src)

def _segment_sum(src, seg, n):
    return jax.ops.segment_sum(src, seg, n)
kernel_name = 'mk_gnn_preln_d1_gnn_r8_22fb17'

def setup_inputs(seed: int=0):
    np.random.seed(seed)
    _w = jnp.asarray

    def _rec_inputs():
        import jax
        import jax.numpy as jnp
        _gk = jax.random.key(seed)
        x = -0.000202 + 1 * jax.random.normal(jax.random.fold_in(_gk, 1), (12500, 128), jnp.float32)
        src = jax.random.randint(jax.random.fold_in(_gk, 2), (200000,), 0, 12500, jnp.int32)
        dst = jax.random.randint(jax.random.fold_in(_gk, 3), (200000,), 0, 12500, jnp.int32)
        _o = jnp.argsort(dst, stable=True)
        src = src[_o]
        dst = dst[_o]
        edge_attr_32 = 0.000196303 + 1.00016 * jax.random.normal(jax.random.fold_in(_gk, 11), (200000, 32), jnp.float32)
        return (x, src, dst, edge_attr_32)
    x, src, dst, edge_attr_32 = _rec_inputs()

    def _L0_gnn_setup():
        import jax, jax.numpy as jnp
        import numpy as np
        N, E = (6250, 100000)
        D_IN, HID, H, C, E_DIM = (128, 128, 4, 32, 32)
        key = jax.random.key(seed)
        ks = jax.random.split(key, 16)

        def lin(k, fan_in, fan_out):
            return jax.random.normal(k, (fan_in, fan_out), jnp.float32) / np.sqrt(fan_in)
        return {'x': jax.random.normal(ks[0], (N, D_IN), jnp.float32), 'edge_index': jax.random.randint(ks[1], (2, E), 0, N, jnp.int32), 'edge_attr': jax.random.normal(ks[2], (E, E_DIM), jnp.float32), 'Wq': lin(ks[3], D_IN, HID), 'bq': jnp.zeros((HID,), jnp.float32), 'Wk': lin(ks[4], D_IN, HID), 'bk': jnp.zeros((HID,), jnp.float32), 'Wv': lin(ks[5], D_IN, HID), 'bv': jnp.zeros((HID,), jnp.float32), 'We': lin(ks[6], E_DIM, HID), 'Wskip': lin(ks[7], D_IN, HID), 'bskip': jnp.zeros((HID,), jnp.float32), 'W1': lin(ks[8], HID, HID), 'b1': jnp.zeros((HID,), jnp.float32), 'W2': lin(ks[9], HID, HID), 'b2': jnp.zeros((HID,), jnp.float32)}
    _L0_gnn_all = _L0_gnn_setup()
    _L0_gnn_in = {k: v for k, v in _L0_gnn_all.items() if k in ('Wq', 'bq', 'Wk', 'bk', 'Wv', 'bv', 'We', 'Wskip', 'bskip', 'W1', 'b1', 'W2', 'b2')}
    del _L0_gnn_all
    return {'x': x, 'src': src, 'dst': dst, 'edge_attr_32': edge_attr_32, 'L0_gnn_Wq': _L0_gnn_in['Wq'], 'L0_gnn_bq': _L0_gnn_in['bq'], 'L0_gnn_Wk': _L0_gnn_in['Wk'], 'L0_gnn_bk': _L0_gnn_in['bk'], 'L0_gnn_Wv': _L0_gnn_in['Wv'], 'L0_gnn_bv': _L0_gnn_in['bv'], 'L0_gnn_We': _L0_gnn_in['We'], 'L0_gnn_Wskip': _L0_gnn_in['Wskip'], 'L0_gnn_bskip': _L0_gnn_in['bskip'], 'L0_gnn_W1': _L0_gnn_in['W1'], 'L0_gnn_b1': _L0_gnn_in['b1'], 'L0_gnn_W2': _L0_gnn_in['W2'], 'L0_gnn_b2': _L0_gnn_in['b2']}

def reference(x, src, dst, edge_attr_32, L0_gnn_Wq, L0_gnn_bq, L0_gnn_Wk, L0_gnn_bk, L0_gnn_Wv, L0_gnn_bv, L0_gnn_We, L0_gnn_Wskip, L0_gnn_bskip, L0_gnn_W1, L0_gnn_b1, L0_gnn_W2, L0_gnn_b2):
    import jax
    import jax.numpy as jnp

    def _L0_gnn_ref(x, edge_index, edge_attr, Wq, bq, Wk, bk, Wv, bv, We, Wskip, bskip, W1, b1, W2, b2):
        import jax, jax.numpy as jnp
        import numpy as np
        N, E = (6250, 100000)
        D_IN, HID, H, C, E_DIM = (128, 128, 4, 32, 32)
        src, dst = (edge_index[0], edge_index[1])
        n = x.shape[0]
        q = (x @ Wq + bq).reshape(n, H, C)
        k = (x @ Wk + bk).reshape(n, H, C)
        v = (x @ Wv + bv).reshape(n, H, C)
        e = (edge_attr @ We).reshape(-1, H, C)
        kj = k[src] + e
        vj = v[src] + e
        alpha = jnp.einsum('ehc,ehc->eh', q[dst], kj) / np.sqrt(C)
        amax = jax.ops.segment_max(alpha, dst, num_segments=n)
        amax = jnp.where(jnp.isfinite(amax), amax, 0.0)
        ex = jnp.exp(alpha - amax[dst])
        denom = jax.ops.segment_sum(ex, dst, num_segments=n)
        alpha = ex / (denom[dst] + 1e-16)
        agg = jax.ops.segment_sum(vj * alpha[:, :, None], dst, num_segments=n)
        out = agg.reshape(n, HID) + (x @ Wskip + bskip)
        h = jax.nn.gelu(out @ W1 + b1, approximate=True)
        h = jax.nn.gelu(h @ W2 + b2, approximate=True)
        return out + h
    edge_index = jnp.stack([src, dst])
    h = jnp.maximum(_layernorm(x, axis=-1), 0.0)
    x = x + _L0_gnn_ref(h, edge_index, edge_attr_32, L0_gnn_Wq, L0_gnn_bq, L0_gnn_Wk, L0_gnn_bk, L0_gnn_Wv, L0_gnn_bv, L0_gnn_We, L0_gnn_Wskip, L0_gnn_bskip, L0_gnn_W1, L0_gnn_b1, L0_gnn_W2, L0_gnn_b2)
    return x

_drawn_inputs = setup_inputs


def setup_inputs(seed=0):
    import zlib

    import numpy as np

    out = dict(_drawn_inputs(seed))
    spreads = {'L0_gnn_bq': (0.0, 0.275),
     'L0_gnn_bk': (0.0, 0.8),
     'L0_gnn_bv': (0.0, 0.1),
     'L0_gnn_bskip': (0.0, 0.1),
     'L0_gnn_b1': (0.0, 0.1),
     'L0_gnn_b2': (0.0, 0.1)}
    factors = {}
    for name, (base, spread) in spreads.items():
        noise = np.random.default_rng([zlib.crc32(name.encode()), seed]).standard_normal(out[name].shape)
        drawn = base * np.exp(spread * noise) if base else spread * noise
        out[name] = jnp.asarray(drawn.astype(out[name].dtype))
    for name, factor in factors.items():
        out[name] = (out[name] * factor).astype(out[name].dtype)
    return out
```

```python
from contextlib import ExitStack

import concourse.bass as bass
from concourse import mybir

F32 = mybir.dt.float32
I32 = mybir.dt.int32
ALU = mybir.AluOpType
ACT = mybir.ActivationFunctionType
AX = mybir.AxisListType
EngineType = mybir.EngineType

P = 128
N, E, D, H, A = 12500, 200000, 128, 4, 32
C = D // H
CW = C + 1
NB = -(-N // P)
NT = -(-E // P)
GI = 4
BI = 32
GB = BI // GI
NBATCH = -(-(NT + NB - 1) // BI)
NI = NBATCH * BI
NC = NI // P
NG = NI // GI
SLOTS = 4
RING = 2 * GB
LAG = GB + GB // 2
PAD = 1 << 14
BIG = 1.0e30
SCALE = float(C) ** -0.5
EPS_LN, EPS_SUM = 1e-5, 1e-16
TAIL0 = (NBATCH - 4) * BI - NB
NTAIL = NI - (NBATCH - 4) * BI + NB
CB = 7
NCH = NB // CB


def wait(engine, semaphore, value):
    if not isinstance(value, int) or value > 0:
        engine.wait_ge(semaphore, value)


def wait_apart(engine, reached, *waits):
    for semaphore, value in waits:
        if not isinstance(value, int):
            engine.to_reg(value)
    engine.wait_ge(reached, 1)
    for semaphore, value in waits:
        wait(engine, semaphore, value)


def live(group):
    return not isinstance(group, int) or 0 <= group < NG


def index_and_nodes(nc, x, src, dst, attr, wq, bq, wk, bk, wv, bv, wskip, bskip, dram, qt, acc, ident, brow):
    kv_dram, skip_dram, dst_dram, src_dram, tag_dram, pen_dram, cp_dram, erec_dram, brow_dram, tail_dram = dram
    NQ = 4 * D
    FULL = (NT // P) * P
    REST = E // P - FULL
    LAST = E - (FULL + REST) * P

    with ExitStack() as ctx:
        def sb(name, shape, dt=F32):
            return ctx.enter_context(nc.sbuf_tensor(name, shape, dt))

        def sem(name):
            return ctx.enter_context(nc.semaphore(name))

        flat, used = acc[:].rearrange("p b f -> p (b f)"), [0]

        def part(shape):
            at, size = used[0], shape[0] * shape[1]
            used[0] += size
            return flat[:, at:at + size].rearrange("p (a b) -> p a b", a=shape[0])

        xs = sb("xs", [P, 2, CB, D])
        w4 = sb("w4", [P, NQ])
        bias4 = sb("bias4", [P, NQ])
        stats = sb("stats", [P, 2, CB, 6])
        mv = sb("mv", [P, 2, CB, 2])
        std = sb("std", [P, 2, CB])
        rstd = sb("rstd", [P, 2, CB])
        eps = sb("eps", [P, 1])
        xn = sb("xn", [P, 2, D])
        ht = sb("ht", [P, 2, P])
        kvs = sb("kvs", [P, 2, CB, 2 * D])
        sks = sb("sks", [P, 2, CB, D])

        dt_i = sb("dt_i", [P, NC, P], I32)
        st_i = sb("st_i", [P, NC, P], I32)
        di_i = sb("di_i", [P, NC, P], I32)
        si_i = sb("si_i", [P, NC, P], I32)
        di = part([NC, P])
        si = part([NC, P])
        ndl = sb("ndl", [P, NC, P])
        tag = part([NC, P])
        tagp = part([NC, P])
        tagn = part([NC, P])
        lastd = sb("lastd", [P, NC])
        kint = sb("kint", [P, NB], I32)
        kf = sb("kf", [P, NB])
        k128 = sb("k128", [P, NB])
        iint = sb("iint", [P, NC], I32)
        ifl = sb("ifl", [P, NC])
        cmp1 = part([NB, NC])
        cmp2 = part([NC, NB])
        cnt = sb("cnt", [P, NB])
        start = sb("start", [P, NB])
        ones = sb("ones", [P, P])
        bsum = sb("bsum", [P, NC])
        bf = sb("bf", [P, NC])
        b128 = sb("b128", [P, NC])
        tf = sb("tf", [P, NC])
        ti = sb("ti", [P, NC], I32)
        cp = sb("cp", [P, 2, NC])
        cpx = sb("cpx", [NC, 2, 4, H, CW])
        bti = sb("bti", [NC, P], I32)
        cap = sb("cap", [1, 1])
        erec = sb("erec", [P, NC, 4, 2 * BI], I32)

        with ExitStack() as pctx:
            def pb(name, shape):
                return pctx.enter_context(nc.psum_tensor(name, shape, F32))

            p_t = [pb(f"p_t{i}", [P, 512]) for i in range(2)]
            p_q = [pb(f"p_q{i}", [P, NQ]) for i in range(2)]
            p_i = pb("p_i", [P, 512])

            x_in = [sem(f"x_in{i}") for i in range(2)]
            w_in = sem("w_in")
            stored = [sem(f"stored{i}") for i in range(2)]
            d_in, s_in = sem("d_in"), sem("s_in")
            scratch_out = sem("scratch_out")
            di_in, si_in = sem("di_in"), sem("si_in")
            tag_out, tagp_in, pen_out, idx_out, brow_out, brow_in, tail_out = (
                sem(n) for n in ("tag_out", "tagp_in", "pen_out", "idx_out", "brow_out", "brow_in", "tail_out"))
            pads, consts, iotas, caps = sem("pads"), sem("consts"), sem("iotas"), sem("caps")
            chain = sem("index_chain")
            cnt_ready, count_ps, ti_ready, tag_ready, pen_ready, tagn_pen, cp_ready = (
                sem(n) for n in ("cnt_ready", "count_ps", "ti_ready", "tag_ready", "pen_ready", "tagn_pen", "cp_ready"))
            si_f, tr_ps, tr_sb, small_ps, small_sb = (sem(n) for n in ("si_f", "tr_ps", "tr_sb", "small_ps", "small_sb"))
            stats_done, aggr_done, std_done, rstd_done = (sem(n) for n in ("stats_done", "aggr_done", "std_done", "rstd_done"))
            xn_ready, xt_ps, ht_ready, qkvs_ps, qkvs_out = (sem(n) for n in ("xn_ready", "xt_ps", "ht_ready", "qkvs_ps", "qkvs_out"))
            block = pctx.enter_context(nc.Block())

            @block.sync
            def _(sp):
                sp.dma_start(dt_i[:, 0:NC - 1, :], dst[0:FULL * P].rearrange("(c p e) -> p c e", p=P, e=P)).then_inc(d_in, 16)
                sp.dma_start(st_i[:, 0:NC - 1, :], src[0:FULL * P].rearrange("(c p e) -> p c e", p=P, e=P)).then_inc(s_in, 16)
                for i, w in enumerate((wk, wv, wq, wskip)):
                    sp.dma_start(w4[:, i * D:(i + 1) * D], w).then_inc(w_in, 16)
                for i, b in enumerate((bk, bv, bq, bskip)):
                    sp.dma_start(bias4[:, i * D:(i + 1) * D],
                                 b.rearrange("(a c) -> a c", a=1).broadcast_to([P, D])).then_inc(w_in, 16)

                def load_x(c, ch):
                    wait(sp, xn_ready, (c - 1) * CB)
                    sp.dma_start(xs[:, ch, :, :], x[bass.ds(c * (CB * P), CB * P), :].rearrange("(u p) d -> p u d", p=P)
                                 ).then_inc(x_in[ch], 16)

                def store_nodes(c, ch):
                    sp.wait_ge(qkvs_out, (c + 1) * CB)
                    rows = bass.ds(c * (CB * P), CB * P)
                    sp.dma_start(kv_dram[rows, :].rearrange("(u p) d -> p u d", p=P), kvs[:, ch, :, :]).then_inc(stored[ch], 16)
                    sp.dma_start(skip_dram[rows, :].rearrange("(u p) d -> p u d", p=P), sks[:, ch, :, :]).then_inc(stored[ch], 16)

                load_x(0, 0)
                load_x(1, 1)
                sp.wait_ge(pads, 1)
                sp.dma_start(dt_i[0:REST, NC - 1, :], dst[FULL * P:(FULL + REST) * P].rearrange("(p e) -> p e", e=P)).then_inc(d_in, 16)
                sp.dma_start(dt_i[REST:REST + 1, NC - 1, 0:LAST], dst[(FULL + REST) * P:E].rearrange("(p e) -> p e", p=1)).then_inc(d_in, 16)
                sp.wait_ge(pads, 2)
                sp.dma_start(st_i[0:REST, NC - 1, :], src[FULL * P:(FULL + REST) * P].rearrange("(p e) -> p e", e=P)).then_inc(s_in, 16)
                sp.dma_start(st_i[REST:REST + 1, NC - 1, 0:LAST], src[(FULL + REST) * P:E].rearrange("(p e) -> p e", p=1)).then_inc(s_in, 16)
                sp.wait_ge(d_in, 48)
                sp.dma_start(dst_dram.rearrange("(c p) e -> p c e", p=P), dt_i[:]).then_inc(scratch_out, 16)
                sp.wait_ge(s_in, 48)
                sp.dma_start(src_dram.rearrange("(c p) e -> p c e", p=P), st_i[:]).then_inc(scratch_out, 16)
                rows = E - TAIL0 * P
                sp.dma_start(tail_dram[0:rows, :], attr[TAIL0 * P:E, :]).then_inc(tail_out, 16)
                sp.dma_start(tail_dram[rows:NTAIL * P, :], attr[0:NTAIL * P - rows, :]).then_inc(tail_out, 16)

                with sp.Fori(0, NCH // 2 - 2) as it:
                    for ch in range(2):
                        load_x(2 * it + 2 + ch, ch)
                        store_nodes(2 * it + ch, ch)
                load_x(NCH - 2, 0)
                store_nodes(NCH - 4, 0)
                r0, r1 = (NB - CB) * P, (NB - 1) * P
                sp.wait_ge(xn_ready, (NCH - 2) * CB)
                sp.dma_start(xs[:, 1, 0:CB - 1, :], x[r0:r1, :].rearrange("(u p) d -> p u d", p=P)).then_inc(x_in[1], 16)
                sp.dma_start(xs[0:N - r1, 1, CB - 1, :], x[r1:N, :]).then_inc(x_in[1], 16)
                store_nodes(NCH - 3, 1)
                store_nodes(NCH - 2, 0)
                sp.wait_ge(qkvs_out, NB)
                for dram_t, s in ((kv_dram, kvs), (skip_dram, sks)):
                    sp.dma_start(dram_t[r0:r1, :].rearrange("(u p) d -> p u d", p=P), s[:, 1, 0:CB - 1, :]).then_inc(stored[1], 16)
                    sp.dma_start(dram_t[r1:N, :], s[0:N - r1, 1, CB - 1, :]).then_inc(stored[1], 16)

                sp.wait_ge(tag_ready, 1)
                sp.wait_ge(caps, 1)
                sp.dma_start(tag_dram[1:1 + NI * P].rearrange("(c p e) -> p c e", p=P, e=P), tag).then_inc(tag_out, 16)
                sp.dma_start(tag_dram[0:1].rearrange("(a e) -> a e", a=1), cap[0:1, 0:1]).then_inc(tag_out, 16)
                sp.dma_start(tag_dram[1 + NI * P:2 + NI * P].rearrange("(a e) -> a e", a=1), cap[0:1, 0:1]).then_inc(tag_out, 16)
                sp.wait_ge(tag_out, 48)
                sp.dma_start(tagp, tag_dram[0:NI * P].rearrange("(c p e) -> p c e", p=P, e=P)).then_inc(tagp_in, 16)
                sp.dma_start(tagn, tag_dram[2:2 + NI * P].rearrange("(c p e) -> p c e", p=P, e=P)).then_inc(tagp_in, 16)
                sp.wait_ge(pen_ready, 1)
                sp.dma_start(pen_dram[:, 0:P].rearrange("(c p) e -> p c e", p=P), tagp).then_inc(pen_out, 16)
                sp.wait_ge(tagn_pen, 1)
                sp.dma_start(pen_dram[:, P:P + 1].rearrange("(c p) e -> p c e", p=P), tagn[:, :, P - 1:P],
                             allow_slow_non_contiguous=True).then_inc(pen_out, 16)
                sp.wait_ge(small_sb, 1)
                sp.dma_start(brow_dram.rearrange("(c i) -> c i", c=NC), bti[:]).then_inc(brow_out, 16)
                sp.wait_ge(brow_out, 16)
                sp.dma_start(brow[:], brow_dram.rearrange("(a i) -> a i", a=1)).then_inc(brow_in, 16)
                sp.wait_ge(small_sb, 3)
                for d in range(2):
                    sp.dma_start(cp_dram[:, d, :].rearrange("(c q) f -> c q f", q=4),
                                 cpx[:, d, :, :, :].rearrange("c q h t -> c q (h t)")).then_inc(idx_out, 16)
                sp.wait_ge(tr_sb, 2 * NC)
                sp.dma_start(erec_dram.rearrange("j e f -> e j f"), erec[:].rearrange("e c q f -> e (c q) f")).then_inc(idx_out, 16)
                sp.wait_ge(idx_out, 48)
                sp.wait_ge(pen_out, 32)
                sp.wait_ge(brow_in, 16)
                sp.wait_ge(tail_out, 32)
                sp.wait_ge(stored[0], 32 * (NCH // 2))
                sp.wait_ge(stored[1], 32 * (NCH // 2 - 1) + 64)

            @block.gpsimd
            def _(pool):
                nc.gpsimd.memset(dt_i[:, NC - 1, :], PAD).then_inc(pads, 1)
                nc.gpsimd.memset(st_i[:, NC - 1, :], 0).then_inc(pads, 1)
                nc.gpsimd.memset(ones[:], 1.0).then_inc(consts, 1)
                nc.gpsimd.memset(ident[:], 0.0).then_inc(consts, 1)
                pool.wait_ge(consts, 2)
                nc.gpsimd.affine_select(out=ident[:], in_=ident[:], compare_op=ALU.not_equal, fill=1.0, base=0,
                                        pattern=[[-1, P]], channel_multiplier=1).then_inc(consts, 1)
                nc.gpsimd.iota(kint[:], pattern=[[1, NB]], base=0, channel_multiplier=0).then_inc(iotas, 1)
                nc.gpsimd.iota(iint[:], pattern=[[P, NC]], base=0, channel_multiplier=1).then_inc(iotas, 1)
                nc.gpsimd.memset(cap[:, 0:1], -1.0).then_inc(caps, 1)
                nc.gpsimd.memset(cpx[:], -BIG).then_inc(caps, 1)
                pool.wait_ge(ti_ready, 1)
                pool.wait_ge(scratch_out, 32)
                for c in range(NC):
                    at = bass.IndirectOffsetOnAxis(ap=ti[:, c:c + 1], axis=0)
                    nc.gpsimd.indirect_dma_start(out=di_i[:, c, :], out_offset=None, in_=dst_dram, in_offset=at).then_inc(di_in, 16)
                for c in range(NC):
                    at = bass.IndirectOffsetOnAxis(ap=ti[:, c:c + 1], axis=0)
                    nc.gpsimd.indirect_dma_start(out=si_i[:, c, :], out_offset=None, in_=src_dram, in_offset=at).then_inc(si_in, 16)

            @block.vector
            def _(dve):
                V = nc.vector
                done = [0]

                def link(ins):
                    done[0] += 1
                    ins.then_inc(chain, 1)
                    dve.wait_ge(chain, done[0])

                V.memset(eps[:], EPS_LN)
                dve.wait_ge(iotas, 2)
                V.tensor_copy(kf[:], kint[:])
                link(V.tensor_copy(ifl[:], iint[:]))
                dve.wait_ge(d_in, 48)
                V.tensor_copy(lastd[:], dt_i[:, :, P - 1])
                link(V.tensor_scalar(k128[:], kf[:], float(P), None, ALU.mult))
                link(V.tensor_tensor(cmp1, lastd[:].unsqueeze(1).broadcast_to([P, NB, NC]),
                                     k128[:].unsqueeze(2).broadcast_to([P, NB, NC]), ALU.is_lt))
                V.tensor_reduce(cnt[:], cmp1, axis=AX.X, op=ALU.add).then_inc(cnt_ready, 1)
                dve.wait_ge(count_ps, 1)
                link(V.tensor_tensor(start[:], p_i[:, 0:NB], kf[:], ALU.add))
                link(V.tensor_tensor(cmp2, start[:].unsqueeze(1).broadcast_to([P, NC, NB]),
                                     ifl[:].unsqueeze(2).broadcast_to([P, NC, NB]), ALU.is_le))
                link(V.tensor_reduce(bsum[:], cmp2, axis=AX.X, op=ALU.add))
                link(V.tensor_scalar(bf[:], bsum[:], -1.0, None, ALU.add))
                link(V.tensor_tensor(tf[:], ifl[:], bf[:], ALU.subtract))
                V.tensor_scalar(b128[:], bf[:], float(P), None, ALU.mult)
                V.tensor_copy(ti[:], tf[:]).then_inc(ti_ready, 1)

                def add_bias(it, k):
                    n = 2 * CB * it + k
                    ch, v = k // CB, k % CB
                    if v == 0:
                        wait(dve, stored[ch], 32 * it)
                    dve.wait_ge(qkvs_ps, n + 1)
                    pq = p_q[k % 2]
                    V.tensor_tensor(kvs[:, ch, v, :], pq[:, 0:2 * D], bias4[:, 0:2 * D], ALU.add)
                    V.tensor_tensor(qt[:, bass.ds(n, 1), :].rearrange("p a d -> p (a d)"), pq[:, 2 * D:3 * D], bias4[:, 2 * D:3 * D], ALU.add)
                    V.tensor_tensor(sks[:, ch, v, :], pq[:, 3 * D:NQ], bias4[:, 3 * D:NQ], ALU.add).then_inc(qkvs_out, 1)

                def chunk(it, ch, more, last=False):
                    c = 2 * it + ch
                    nx = 1 - ch
                    for u in range(CB):
                        n = c * CB + u
                        k = ch * CB + u
                        wait(dve, xt_ps, n - 1)
                        if u == 0:
                            dve.wait_ge(rstd_done, c + 1)
                        V.tensor_scalar(xn[:, k % 2, :], xs[:, ch, u, :],
                                        mv[:, ch, u, 0:1], rstd[:, ch, u:u + 1], ALU.subtract, ALU.mult).then_inc(xn_ready, 1)
                        if more:
                            if u == 0:
                                dve.wait_ge(x_in[nx], 16 * (it + 1 + ch) + 16 * (last and ch == 0))
                            V.bn_stats(stats[:, nx, u, :], xs[:, nx, u, :]).then_inc(stats_done, 1)
                        if k >= 2:
                            add_bias(it, k - 2)
                        elif not isinstance(it, int) or it > 0:
                            add_bias(it - 1, k - 2 + 2 * CB)
                        if more:
                            wait_apart(dve, w_in, (stats_done, (c + 1) * CB + u + 1))
                            V.bn_aggr(mv[:, nx, u, :], stats[:, nx, u, :]).then_inc(aggr_done, 1)
                    if more:
                        dve.wait_ge(std_done, c + 2)
                        V.reciprocal(rstd[:, nx, :], std[:, nx, :]).then_inc(rstd_done, 1)

                dve.wait_ge(x_in[0], 16)
                for u in range(CB):
                    V.bn_stats(stats[:, 0, u, :], xs[:, 0, u, :]).then_inc(stats_done, 1)
                for u in range(CB):
                    dve.wait_ge(stats_done, u + 1)
                    V.bn_aggr(mv[:, 0, u, :], stats[:, 0, u, :]).then_inc(aggr_done, 1)
                dve.wait_ge(std_done, 1)
                V.reciprocal(rstd[:, 0, :], std[:, 0, :]).then_inc(rstd_done, 1)
                dve.wait_ge(w_in, 128)
                chunk(0, 0, True)
                chunk(0, 1, True)
                with dve.Fori(1, NCH // 2 - 1) as it:
                    chunk(it, 0, True)
                    chunk(it, 1, True)
                chunk(NCH // 2 - 1, 0, True, last=True)
                chunk(NCH // 2 - 1, 1, False)
                add_bias(NCH // 2 - 1, 2 * CB - 2)
                add_bias(NCH // 2 - 1, 2 * CB - 1)

                dve.wait_ge(di_in, 16 * NC)
                link(V.tensor_copy(di, di_i[:]))
                bcast = b128[:].unsqueeze(2).broadcast_to([P, NC, P])
                V.tensor_scalar(tag, di, float(P), None, ALU.mult).then_inc(chain, 1)
                done[0] += 1
                V.tensor_tensor(ndl[:], bcast, di, ALU.subtract)
                dve.wait_ge(chain, done[0])
                V.tensor_tensor(tag, tag, bf[:].unsqueeze(2).broadcast_to([P, NC, P]), ALU.add).then_inc(tag_ready, 1)
                dve.wait_ge(si_in, 16 * NC)
                V.tensor_copy(si, si_i[:]).then_inc(si_f, 1)
                for n in range(2 * NC):
                    c, which = n // 2, n % 2
                    dve.wait_ge(tr_ps, n + 1)
                    pv = p_t[which][:, 0:P].rearrange("e (q t) -> e q t", q=4)
                    if which == 0:
                        V.tensor_copy(erec[:, c, :, 0:BI], pv).then_inc(tr_sb, 1)
                    else:
                        V.tensor_copy(erec[:, c, :, BI:2 * BI].bitcast(F32), pv).then_inc(tr_sb, 1)
                dve.wait_ge(tagp_in, 32)
                link(V.tensor_tensor(tagp, tag, tagp, ALU.not_equal))
                link(V.tensor_tensor(tagn, tag, tagn, ALU.not_equal))
                V.tensor_scalar(tagp, tagp, -BIG, None, ALU.mult).then_inc(pen_ready, 1)
                V.tensor_scalar(tagn, tagn, -BIG, None, ALU.mult).then_inc(tagn_pen, 1)
                dve.wait_ge(tagn_pen, 1)
                dve.wait_ge(pen_ready, 1)
                V.tensor_reduce(cp[:, 0, :], tagp, axis=AX.X, op=ALU.add).then_inc(cp_ready, 1)
                V.tensor_reduce(cp[:, 1, :], tagn, axis=AX.X, op=ALU.add).then_inc(cp_ready, 1)
                dve.wait_ge(small_ps, 1)
                V.tensor_copy(bti[:], p_i[0:NC, 0:P]).then_inc(small_sb, 1)
                dve.wait_ge(caps, 2)
                for d in range(2):
                    dve.wait_ge(small_ps, 2 + d)
                    V.tensor_copy(cpx[:, d, :, :, (1 - d):(1 - d) + BI],
                                  p_i[0:NC, P * (1 + d):P * (2 + d)].rearrange("c (q t) -> c q t", q=4).unsqueeze(2)
                                  .broadcast_to([NC, 4, H, BI])).then_inc(small_sb, 1)

            @block.scalar
            def _(act):
                S = nc.scalar

                def chunk_std(c, ch):
                    act.wait_ge(aggr_done, (c + 1) * CB)
                    S.activation(std[:, ch, :], mv[:, ch, :, 1], ACT.Sqrt, bias=eps[:, 0:1]).then_inc(std_done, 1)

                def blocks(c, ch):
                    for u in range(CB):
                        n = c * CB + u
                        k = (ch * CB + u)
                        act.wait_ge(xt_ps, n + 1)
                        wait(act, qkvs_ps, n - 1)
                        S.activation(ht[:, k % 2, :], p_t[k % 2][:, 0:P], ACT.Relu).then_inc(ht_ready, 1)

                chunk_std(0, 0)
                for ch in range(2):
                    blocks(ch, ch)
                    chunk_std(ch + 1, 1 - ch)
                with act.Fori(1, NCH // 2 - 1) as it:
                    for ch in range(2):
                        blocks(2 * it + ch, ch)
                        chunk_std(2 * it + ch + 1, 1 - ch)
                blocks(NCH - 2, 0)
                chunk_std(NCH - 1, 1)
                blocks(NCH - 1, 1)

            @block.tensor
            def _(pe):
                T = nc.tensor
                pe.wait_ge(consts, 3)
                pe.wait_ge(cnt_ready, 1)
                T.matmul(p_i[:, 0:NB], ones[:], cnt[:], start=True, stop=True).then_inc(count_ps, 1)
                pe.wait_ge(w_in, 128)

                def transpose(n, k):
                    pe.wait_ge(xn_ready, n + 1)
                    wait(pe, ht_ready, n - 1)
                    T.transpose(p_t[k % 2][:, 0:P], xn[:, k % 2, :], ident[:]).then_inc(xt_ps, 1)

                def product(n, k):
                    pe.wait_ge(ht_ready, n + 1)
                    wait(pe, qkvs_out, n - 1)
                    T.matmul(p_q[k % 2][:], ht[:, k % 2, :], w4[:], start=True, stop=True).then_inc(qkvs_ps, 1)

                def pair(it):
                    for k in range(2 * CB):
                        transpose(2 * CB * it + k, k)
                        if k >= 1:
                            product(2 * CB * it + k - 1, k - 1)
                    product(2 * CB * it + 2 * CB - 1, 2 * CB - 1)

                pair(0)
                with pe.Fori(1, NCH // 2) as it:
                    pair(it)
                pe.wait_ge(si_f, 1)
                for n in range(2 * NC):
                    wait(pe, tr_sb, n - 1)
                    T.transpose(p_t[n % 2][:, 0:P], (si if n % 2 == 0 else ndl)[:, n // 2, :], ident[:]).then_inc(tr_ps, 1)
                T.transpose(p_i[0:NC, 0:P], bf[:], ident[:]).then_inc(small_ps, 1)
                pe.wait_ge(cp_ready, 2)
                for d in range(2):
                    pe.wait_ge(small_sb, 1 + d)
                    T.transpose(p_i[0:NC, P * (1 + d):P * (2 + d)], cp[:, d, :], ident[:]).then_inc(small_ps, 1)


def edges(nc, attr, we, dram, qt, acc, ident, brow):
    kv_dram, skip_dram, dst_dram, src_dram, tag_dram, pen_dram, cp_dram, erec_dram, brow_dram, tail_dram = dram
    UNR = 2 * GB
    TURNS = NG // UNR
    PENS = H + 1
    STEPS_LEFT = LAG + 1

    with ExitStack() as ctx:
        def sb(name, shape, dt=F32):
            return ctx.enter_context(nc.sbuf_tensor(name, shape, dt))

        def pb(name, shape):
            return ctx.enter_context(nc.psum_tensor(name, shape, F32))

        def sem(name):
            return ctx.enter_context(nc.semaphore(name))

        val = sb("val", [P, RING, GI, H, CW])
        onehot = sb("onehot", [P, RING, GI, P])
        kvr = sb("kvr", [P, SLOTS, GI, 2 * D])
        araw = sb("araw", [P, SLOTS, GI, A])
        at = sb("at", [P, P])
        st = sb("st", [P, GI, P])
        we4 = sb("we4", [P, GI, D])
        wv = sb("wv", [P, 2, GI, H * CW])
        alpha = sb("alpha", [P, 2, H, BI])
        ex = sb("ex", [P, 2, H, BI])
        erec = sb("erec2", [P, 2, 2 * BI], I32)
        pen = sb("pen", [P, 2, P + 1])
        fwd = sb("fwd", [P, P])
        bwd = sb("bwd", [P, P])
        cin = sb("cin", [P, 2])
        fac = sb("fac", [P, H])
        iota_f = sb("iota_f", [P, P])
        iota_i = fwd[:, :].bitcast(I32)
        sel4 = sb("sel4", [P, H])
        one = sb("one", [1, 1])
        cpr = sb("cpr", [1, 2, 2, H * CW])
        zf = sb("zf", [1, H, CW])
        rf = sb("rf", [1, H, CW])
        zb = sb("zb", [1, H, CW])
        dm = sb("dm", [1, 2, H])

        p_e = pb("p_e", [P, 512])
        p_qd = pb("p_qd", [P, 512])
        p_st = pb("p_st", [P, 512])
        p_ag = [pb(f"p_ag{i}", [P, 512]) for i in range(2)]
        p_at = pb("p_at", [P, 512])
        p_al = pb("p_al", [P, 512])
        p_sm = pb("p_sm", [P, 512])
        p_row, p_col, p_m, p_f = p_sm[0:1, 0:P], p_sm[:, P:P + 1], p_sm[0:1, 132:132 + H], p_sm[:, 140:140 + H]
        p_ex = p_al[:, 256:256 + P]

        kv_in = [sem(f"kv_in{i}") for i in range(SLOTS)]
        attr_in = [sem(f"attr_in{i}") for i in range(SLOTS)]
        erec_in = [sem(f"erec_in{i}") for i in range(2)]
        pen_in = [sem(f"pen_in{i}") for i in range(2)]
        we_in, setup = sem("we_in"), sem("setup")
        at_ps, at_sb, st_ps, st_sb, sq_done, onehot_done = (sem(n) for n in ("at_ps", "at_sb", "st_ps", "st_sb", "sq_done", "onehot_done"))
        e_ps, q_ps, k_done, v_done, prod_done, alpha_done = (sem(n) for n in ("e_ps", "q_ps", "k_done", "v_done", "prod_done", "alpha_done"))
        wv_done, agg_ps, acc_done, scaled = (sem(n) for n in ("wv_done", "agg_ps", "acc_done", "scaled"))
        al_ps, last_f, row_f, carry_f, z_f, run_f, col_f, cin_f, fwd_done = (
            sem(n) for n in ("al_ps", "last_f", "row_f", "carry_f", "z_f", "run_f", "col_f", "cin_f", "fwd_done"))
        first_b, row_b, z_b, run_b, col_b, cin_b, max_done = (
            sem(n) for n in ("first_b", "row_b", "z_b", "run_b", "col_b", "cin_b", "max_done"))
        diff_done, ext_done, ex_ps, ex_done, m_ps, dm_sub, dm_done, f_ps, f_done = (
            sem(n) for n in ("diff_done", "ext_done", "ex_ps", "ex_done", "m_ps", "dm_sub", "dm_done", "f_ps", "f_done"))
        block = ctx.enter_context(nc.Block())

        def blocks_of(engine, n):
            return nc.values_load_multi_w_load_instructions(
                brow[0:1, bass.ds(GI * n, GI)], engines=[engine], min_val=0, max_val=NB - 1,
                skip_runtime_bounds_check_because="b[i] counts blocks started, out of NB")[1]

        def behind(turn, s):
            j = 2 * turn + s // GB - 1
            return (j, (s // GB + 1) % 2) if not isinstance(j, int) or 0 <= j < NBATCH else (None, None)

        @block.sync
        def _(sp):
            sp.wait_ge(setup, 1)
            for i in range(GI):
                sp.dma_start(we4[A * i:A * (i + 1), i, :], we).then_inc(we_in, 16)

            def load_items(j, jj):
                wait(sp, alpha_done, GB * (j - 1))
                sp.dma_start(erec[:, jj, :], erec_dram[bass.ds(j, 1), :, :].rearrange("a e f -> (a e) f")).then_inc(erec_in[jj], 16)

            def load_pens(j, jj):
                wait(sp, max_done, j - 1)
                wait(sp, run_b, j - 1)
                for h in range(H):
                    sp.dma_start(pen[BI * h:BI * (h + 1), jj, :], pen_dram[bass.ds(j * BI, BI), :]).then_inc(pen_in[jj], 16)
                sp.dma_start(cpr[0:1, jj, :, :].rearrange("a d f -> a (d f)"),
                             cp_dram[bass.ds(j, 1), :, :].rearrange("a d f -> a (d f)")).then_inc(pen_in[jj], 16)

            def step(turn, s, table, tile0):
                n = UNR * turn + s
                jj = s // GB
                j = 2 * turn + jj
                wait(sp, at_ps, n - SLOTS + 1)
                blocks = blocks_of(EngineType.SP, n)
                for i in range(GI):
                    tile = nc.s_assert_within(GI * n + i - blocks[i] - tile0, 0, table.shape[0] // P - 1, skip_runtime_bounds_check_because=(
                        "item i's tile is i - b[i], from 0 to the tile that item i would have with b = 0"))
                    sp.dma_start(araw[:, s % SLOTS, i, :], table[bass.ds(tile * P, P), :]).then_inc(attr_in[s % SLOTS], 16)
                if s % GB == 3:
                    load_pens(j, jj)
                if s % GB == 5 and not (isinstance(j, int) and j + 1 >= NBATCH):
                    load_items(j + 1, 1 - jj)

            load_items(0, 0)
            for s in range(UNR):
                step(0, s, attr, 0)
            whole = (NBATCH - 4) // 2
            with sp.Fori(1, whole) as turn:
                for s in range(UNR):
                    step(turn, s, attr, 0)
            for turn in range(whole, TURNS):
                for s in range(UNR):
                    step(turn, s, tail_dram, TAIL0)

        @block.gpsimd
        def _(pool):
            nc.gpsimd.memset(we4[:], 0.0).then_inc(setup, 1)
            nc.gpsimd.iota(iota_i, pattern=[[1, P]], base=0, channel_multiplier=0).then_inc(setup, 1)
            nc.gpsimd.memset(sel4[:], 0.0).then_inc(setup, 1)
            nc.gpsimd.memset(one[:], 1.0).then_inc(setup, 1)
            nc.gpsimd.memset(zb[:], -BIG).then_inc(setup, 1)
            nc.gpsimd.memset(rf[:], -BIG).then_inc(setup, 1)
            pool.wait_ge(setup, 6)
            nc.gpsimd.tensor_copy(iota_f[:], iota_i).then_inc(setup, 1)
            nc.gpsimd.affine_select(out=sel4[:], in_=sel4[:], compare_op=ALU.not_equal, fill=1.0, base=0,
                                    pattern=[[-BI, H]], channel_multiplier=1).then_inc(setup, 1)
            nc.gpsimd.memset(val[:, :, :, :, C:CW], 1.0).then_inc(setup, 1)
            nc.gpsimd.memset(acc[:], 0.0).then_inc(setup, 1)

            def step(turn, s):
                n = UNR * turn + s
                jj = s // GB
                batch = ((erec_in[jj], 16 * (turn + 1)),) if s % GB == 0 else ()
                wait_apart(pool, setup, (alpha_done, n - SLOTS + 1), *batch)
                for i in range(GI):
                    t = GI * (s % GB) + i
                    nc.gpsimd.indirect_dma_start(
                        out=kvr[:, s % SLOTS, i, :], out_offset=None, in_=kv_dram,
                        in_offset=bass.IndirectOffsetOnAxis(ap=erec[:, jj, t:t + 1], axis=0)).then_inc(kv_in[s % SLOTS], 16)

            for s in range(UNR):
                step(0, s)
            with pool.Fori(1, TURNS) as turn:
                for s in range(UNR):
                    step(turn, s)

        @block.vector
        def _(dve):
            V = nc.vector

            def add_item(turn, s, i, blocks):
                n = UNR * turn + s - LAG - 1
                if not live(n):
                    return
                first = (s - LAG - 1) % GB == 0
                if i == 0:
                    if first:
                        j = 2 * turn + (s - LAG - 1) // GB
                        wait(dve, acc_done, GI * n)
                        dve.wait_ge(f_done, j + 1)
                        rows = acc[:, bass.ds(blocks[0], 1), :].rearrange("p a (h c) -> p (a h) c", c=CW)
                        V.tensor_tensor(rows, rows, fac[:].unsqueeze(2).broadcast_to([P, H, CW]), ALU.mult).then_inc(scaled, 1)
                if i == 0:
                    dve.wait_ge(agg_ps, n + 1)
                    if first:
                        dve.wait_ge(scaled, j + 1)
                wait(dve, acc_done, GI * n + i)
                rows = acc[:, bass.ds(blocks[i], 1), :].rearrange("p a f -> p (a f)")
                V.tensor_tensor(rows, rows, p_ag[i // 2][:, (i % 2) * 256:(i % 2) * 256 + H * CW], ALU.add).then_inc(acc_done, 1)

            def softmax(turn, s, place):
                j, jj = behind(turn, s)
                if j is None:
                    return
                at_ = (s % GB, place)
                al = p_al[:, 0:P]
                if at_ == (0, 0):
                    dve.wait_ge(al_ps, j + 1)
                    wait(dve, ex_ps, j)
                    dve.wait_ge(pen_in[jj], 16 * PENS * (turn + s // GB))
                    V.tensor_tensor_scan(fwd[:], pen[:, jj, 0:P], al, -BIG, ALU.add, ALU.max).then_inc(last_f, 1)
                    V.tensor_copy(zf[:, :, 0], rf[:, :, BI]).then_inc(carry_f, 1)
                elif at_ == (0, 1):
                    dve.wait_ge(row_f, j + 1)
                    V.tensor_copy(zf[:, :, 1:CW], p_row.rearrange("a (h t) -> a h t", h=H)).then_inc(z_f, 1)
                elif at_ == (0, 2):
                    dve.wait_ge(carry_f, j + 1)
                    dve.wait_ge(z_f, j + 1)
                    V.tensor_tensor_scan(rf[:].rearrange("a h t -> a (h t)"), cpr[0:1, jj, 0, :],
                                         zf[:].rearrange("a h t -> a (h t)"), -BIG, ALU.add, ALU.max).then_inc(run_f, 1)
                elif at_ == (1, 0):
                    dve.wait_ge(col_f, j + 1)
                    V.tensor_copy(cin[:, 0:1], p_col).then_inc(cin_f, 1)
                elif at_ == (1, 1):
                    dve.wait_ge(cin_f, j + 1)
                    V.tensor_tensor_scan(fwd[:], pen[:, jj, 0:P], al, cin[:, 0:1], ALU.add, ALU.max).then_inc(fwd_done, 1)
                elif at_ == (1, 2):
                    dve.wait_ge(fwd_done, j + 1)
                    V.tensor_tensor_scan(bwd[:, ::-1], pen[:, jj, P:0:-1], fwd[:, ::-1], -BIG, ALU.add, ALU.max).then_inc(first_b, 1)
                elif at_ == (2, 0):
                    dve.wait_ge(row_b, j + 1)
                    V.tensor_copy(zb[:, :, 0:BI], p_row.rearrange("a (h t) -> a h t", h=H)).then_inc(z_b, 1)
                elif at_ == (2, 1):
                    dve.wait_ge(z_b, j + 1)
                    V.tensor_tensor_scan(zb[:].rearrange("a h t -> a (h t)")[:, ::-1], cpr[0:1, jj, 1, ::-1],
                                         zb[:].rearrange("a h t -> a (h t)")[:, ::-1], -BIG, ALU.add, ALU.max).then_inc(run_b, 1)
                elif at_ == (3, 0):
                    dve.wait_ge(col_b, j + 1)
                    V.tensor_copy(cin[:, 1:2], p_col).then_inc(cin_b, 1)
                elif at_ == (3, 1):
                    dve.wait_ge(cin_b, j + 1)
                    V.tensor_tensor_scan(bwd[:, ::-1], pen[:, jj, P:0:-1], fwd[:, ::-1], cin[:, 1:2], ALU.add, ALU.max).then_inc(max_done, 1)
                elif at_ == (3, 2):
                    dve.wait_ge(max_done, j + 1)
                    V.tensor_tensor(fwd[:], al, bwd[:], ALU.subtract).then_inc(diff_done, 1)
                elif at_ == (4, 0):
                    dve.wait_ge(m_ps, j + 1)
                    V.tensor_tensor(dm[:, 0, :], zf[:, :, 0], p_m, ALU.subtract).then_inc(dm_sub, 1)
                elif at_ == (4, 1):
                    dve.wait_ge(dm_sub, j + 1)
                    V.tensor_scalar(dm[:, 1, :], dm[:, 0, :], 0.0, None, ALU.min).then_inc(dm_done, 1)

            def step(turn, s):
                n = UNR * turn + s
                jj = s // GB
                j = 2 * turn + jj
                slot = s % SLOTS
                here = live(n)
                kpart = kvr[:, slot, :, 0:D]
                blocks = blocks_of(EngineType.DVE, n - LAG - 1) if live(n - LAG - 1) else None
                if here:
                    dve.wait_ge(kv_in[slot], 16 * GI * (UNR // SLOTS * turn + s // SLOTS + 1))
                    dve.wait_ge(e_ps, n + 1)
                    pe_ = p_e[:].rearrange("e (i c) -> e i c", i=GI)
                    V.tensor_tensor(kpart, kpart, pe_, ALU.add).then_inc(k_done, 1)
                add_item(turn, s, 0, blocks)
                if here:
                    V.tensor_tensor(val[:, s % RING, :, :, 0:C], kvr[:, slot, :, D:2 * D].rearrange("e i (h c) -> e i h c", h=H),
                                    p_e[:].rearrange("e (i h c) -> e i h c", i=GI, h=H), ALU.add).then_inc(v_done, 1)
                add_item(turn, s, 1, blocks)
                softmax(turn, s, 0)
                if here:
                    dve.wait_ge(q_ps, n + 1)
                    dve.wait_ge(k_done, n + 1)
                    V.tensor_tensor(kpart, kpart, p_qd[:].rearrange("e (i c) -> e i c", i=GI), ALU.mult).then_inc(prod_done, 1)
                add_item(turn, s, 2, blocks)
                m = n - LAG
                if live(m):
                    sm = (s - LAG) % RING
                    jb = 2 * turn + (s - LAG) // GB
                    t0 = GI * ((s - LAG) % GB)
                    dve.wait_ge(ex_done, jb + 1)
                    wait(dve, agg_ps, m - 1)
                    dve.wait_ge(v_done, m + 1)
                    V.tensor_tensor(wv[:, s % 2, :, :].rearrange("e i (h c) -> e i h c", h=H), val[:, sm, :, :, :],
                                    ex[:, ((s - LAG) // GB) % 2, :, t0:t0 + GI].rearrange("e h i -> e i h").unsqueeze(3)
                                    .broadcast_to([P, GI, H, CW]), ALU.mult).then_inc(wv_done, 1)
                softmax(turn, s, 1)
                add_item(turn, s, 3, blocks)
                if here:
                    dve.wait_ge(prod_done, n + 1)
                    if s % GB == 0:
                        wait(dve, al_ps, j - 1)
                    t0 = GI * (s % GB)
                    V.tensor_reduce(alpha[:, jj, :, t0:t0 + GI].rearrange("e h i -> e i h"),
                                    kpart.rearrange("e i (h c) -> e i h c", h=H), axis=AX.X, op=ALU.add).then_inc(alpha_done, 1)
                softmax(turn, s, 2)

            dve.wait_ge(setup, 10)
            for s in range(UNR):
                step(0, s)
            with dve.Fori(1, TURNS) as turn:
                for s in range(UNR):
                    step(turn, s)
            for s in range(STEPS_LEFT):
                step(TURNS, s)

        @block.scalar
        def _(act):
            S = nc.scalar

            def one_hots(turn, s):
                n = UNR * turn + s
                if not live(n):
                    return
                jj = (s // GB) % 2
                slot = s % RING
                act.wait_ge(erec_in[jj], 16 * (turn + s // UNR + 1))
                wait(act, agg_ps, n - RING + 1)
                for i in range(GI):
                    t = BI + GI * (s % GB) + i
                    last = S.activation(onehot[:, slot, i, :], iota_f[:], ACT.Square, bias=erec[:, jj, t:t + 1].bitcast(F32))
                last.then_inc(sq_done, 1)
                act.wait_ge(sq_done, n + 1)
                S.activation(onehot[:, slot, :, :], onehot[:, slot, :, :], ACT.Relu, scale=-1.0, bias=1.0).then_inc(onehot_done, 1)

            def copies(turn, s):
                n = UNR * turn + s
                if not live(n):
                    return
                act.wait_ge(at_ps, n + 1)
                wait(act, e_ps, n)
                S.activation(at[:], p_at[:, 0:P], ACT.Copy).then_inc(at_sb, 1)
                act.wait_ge(st_ps, n + 1)
                wait(act, q_ps, n)
                S.activation(st[:].rearrange("p i e -> p (i e)"), p_st[:], ACT.Copy).then_inc(st_sb, 1)

            def step(turn, s):
                j, jj = behind(turn, s)
                if s % GB == 4 and j is not None:
                    act.wait_ge(diff_done, j + 1)
                    S.activation(fwd[:], fwd[:], ACT.Exp, scale=SCALE).then_inc(ext_done, 1)
                    act.wait_ge(ex_ps, j + 1)
                    wait(act, wv_done, GB * (j - 1))
                    S.activation(ex[:, jj, :, :].rearrange("e h t -> e (h t)"), p_ex, ACT.Copy).then_inc(ex_done, 1)
                copies(turn, s + 1)
                one_hots(turn, s + 2)
                if s % GB == 4 and j is not None:
                    act.wait_ge(f_ps, j + 1)
                    wait(act, scaled, j)
                    S.activation(fac[:], p_f, ACT.Exp, scale=SCALE).then_inc(f_done, 1)

            act.wait_ge(setup, 7)
            one_hots(0, 0)
            copies(0, 0)
            one_hots(0, 1)
            for s in range(UNR):
                step(0, s)
            with act.Fori(1, TURNS - 1) as turn:
                for s in range(UNR):
                    step(turn, s)
            for s in range(UNR):
                step(TURNS - 1, s)
            for s in range(STEPS_LEFT):
                step(TURNS, s)

        @block.tensor
        def _(pe):
            T = nc.tensor

            def transposes(turn, s):
                n = UNR * turn + s
                if not live(n):
                    return
                slot = s % SLOTS
                pe.wait_ge(attr_in[slot], 16 * GI * (UNR // SLOTS * turn + s // SLOTS + 1))
                wait(pe, at_sb, n)
                T.transpose(p_at[:, 0:P], araw[:, slot, :, :].rearrange("e i a -> e (i a)"), ident[:]).then_inc(at_ps, 1)
                pe.wait_ge(onehot_done, n + 1)
                wait(pe, st_sb, n)
                for i in range(GI):
                    last = T.transpose(p_st[:, i * P:(i + 1) * P], onehot[:, s % RING, i, :], ident[:])
                last.then_inc(st_ps, 1)

            def edge_terms(turn, s):
                n = UNR * turn + s
                if not live(n):
                    return
                pe.wait_ge(at_sb, n + 1)
                wait(pe, v_done, n)
                T.matmul(p_e[:], at[:], we4[:].rearrange("a i c -> a (i c)"), start=True, stop=True).then_inc(e_ps, 1)

            def queries(turn, s):
                n = UNR * turn + s
                if not live(n):
                    return
                blocks = blocks_of(EngineType.PE, n)
                pe.wait_ge(st_sb, n + 1)
                wait(pe, prod_done, n)
                for i in range(GI):
                    last = T.matmul(p_qd[:, i * P:(i + 1) * P], st[:, i, :], qt[:, bass.ds(blocks[i], 1), :].rearrange("p a d -> p (a d)"),
                                    start=True, stop=True)
                last.then_inc(q_ps, 1)

            def sums(turn, s):
                n = UNR * turn + s
                if not live(n):
                    return
                pe.wait_ge(wv_done, n + 1)
                wait(pe, acc_done, GI * n)
                for i in range(GI):
                    last = T.matmul(p_ag[i // 2][:, (i % 2) * 256:(i % 2) * 256 + H * CW], onehot[:, s % RING, i, :],
                                    wv[:, s % 2, i, :], start=True, stop=True)
                last.then_inc(agg_ps, 1)

            def softmax(turn, s, place):
                j, jj = behind(turn, s)
                if j is None:
                    return
                at_ = (s % GB, place)
                if at_ == (0, 0):
                    pe.wait_ge(alpha_done, GB * (j + 1))
                    wait(pe, ex_done, j)
                    T.transpose(p_al[:, 0:P], alpha[:, jj, :, :].rearrange("e h t -> e (h t)"), ident[:]).then_inc(al_ps, 1)
                elif at_ == (0, 1):
                    pe.wait_ge(last_f, j + 1)
                    wait(pe, f_done, j)
                    T.matmul(p_row, fwd[:, P - 1:P], ident[:], start=True, stop=True).then_inc(row_f, 1)
                elif at_ == (1, 0):
                    wait_apart(pe, setup, (run_f, j + 1))
                    for h in range(H):
                        last = T.matmul(p_col[BI * h:BI * (h + 1), :], rf[0:1, h, 0:BI], one[:], start=True, stop=True)
                    last.then_inc(col_f, 1)
                elif at_ == (2, 0):
                    pe.wait_ge(first_b, j + 1)
                    T.matmul(p_row, bwd[:, 0:1], ident[:], start=True, stop=True).then_inc(row_b, 1)
                elif at_ == (3, 0):
                    wait_apart(pe, setup, (run_b, j + 1))
                    for h in range(H):
                        last = T.matmul(p_col[BI * h:BI * (h + 1), :], zb[0:1, h, 1:CW], one[:], start=True, stop=True)
                    last.then_inc(col_b, 1)
                elif at_ == (4, 0):
                    pe.wait_ge(max_done, j + 1)
                    T.matmul(p_m, bwd[:, 0:1], sel4[:], start=True, stop=True).then_inc(m_ps, 1)
                    pe.wait_ge(ext_done, j + 1)
                    T.transpose(p_ex, fwd[:], ident[:]).then_inc(ex_ps, 1)
                elif at_ == (4, 2):
                    pe.wait_ge(dm_done, j + 1)
                    T.matmul(p_f, onehot[0:1, jj * GB, 0, :], dm[:, 1, :], start=True, stop=True).then_inc(f_ps, 1)

            def step(turn, s):
                softmax(turn, s, 0)
                transposes(turn, s + 1)
                edge_terms(turn, s + 1)
                softmax(turn, s, 1)
                queries(turn, s + 1)
                sums(turn, s - LAG)
                softmax(turn, s, 2)

            pe.wait_ge(setup, 8)
            pe.wait_ge(we_in, 16 * GI)
            transposes(0, 0)
            edge_terms(0, 0)
            queries(0, 0)
            for s in range(UNR):
                step(0, s)
            with pe.Fori(1, TURNS - 1) as turn:
                for s in range(UNR):
                    step(turn, s)
            for s in range(UNR):
                step(TURNS - 1, s)
            for s in range(STEPS_LEFT):
                step(TURNS, s)


def output(nc, x, w1, b1, w2, b2, out, dram, acc, ident):
    skip_dram = dram[1]
    WID = 4
    GROUPS = NB // WID
    REST = NB - GROUPS * WID

    with ExitStack() as ctx:
        def sb(name, shape, dt=F32):
            return ctx.enter_context(nc.sbuf_tensor(name, shape, dt))

        def sem(name):
            return ctx.enter_context(nc.semaphore(name))

        xs = sb("x3", [P, 2, WID, D])
        sk = sb("skip3", [P, 2, WID, D])
        w1s, w2s = sb("w1s", [P, D]), sb("w2s", [P, D])
        b1s, b2s = sb("b1s", [P, 1]), sb("b2s", [P, 1])
        den = sb("den", [P, 2, WID, H])
        o = sb("o", [P, 2, WID, D])
        ot = sb("ot", [P, WID * P])
        h1 = sb("h1", [P, WID * P])
        h2 = sb("h2", [P, WID * P])
        res = sb("res", [P, 2, WID, D])
        p_o, p_1, p_2, p_3 = (ctx.enter_context(nc.psum_tensor(f"p3_{i}", [P, 512], F32)) for i in range(4))
        loaded = [sem(f"loaded{i}") for i in range(2)]
        w_in3 = sem("w_in3")
        den_add, den_inv, normed, out_ready, xo_ready = (sem(n) for n in ("den_add", "den_inv", "normed", "out_ready", "xo_ready"))
        ot_ps, ot_sb, h1_ps, h1_sb, h2_ps, h2_sb, y_ps, res_ready = (
            sem(n) for n in ("ot_ps", "ot_sb", "h1_ps", "h1_sb", "h2_ps", "h2_sb", "y_ps", "res_ready"))
        out_stored = [sem(f"out_stored{i}") for i in range(2)]
        block = ctx.enter_context(nc.Block())

        @block.sync
        def _(sp):
            sp.dma_start(w1s[:], w1).then_inc(w_in3, 16)
            sp.dma_start(w2s[:], w2).then_inc(w_in3, 16)
            sp.dma_start(b1s[:], b1.rearrange("(c a) -> c a", a=1)).then_inc(w_in3, 16)
            sp.dma_start(b2s[:], b2.rearrange("(c a) -> c a", a=1)).then_inc(w_in3, 16)

            def load(g, k):
                wait(sp, xo_ready, g - 1)
                rows = bass.ds(g * (WID * P), WID * P)
                for t, s in ((xs, x), (sk, skip_dram)):
                    sp.dma_start(t[:, k, :, :], s[rows, :].rearrange("(u p) d -> p u d", p=P)).then_inc(loaded[k], 16)

            def store(g, k):
                sp.wait_ge(res_ready, g + 1)
                sp.dma_start(out[bass.ds(g * (WID * P), WID * P), :].rearrange("(u p) d -> p u d", p=P), res[:, k, :, :]
                             ).then_inc(out_stored[k], 16)

            load(0, 0)
            load(1, 1)
            with sp.Fori(0, GROUPS // 2 - 1) as it:
                for k in range(2):
                    store(2 * it + k, k)
                    load(2 * it + 2 + k, k)
            store(GROUPS - 2, 0)
            r0, r1 = GROUPS * WID * P, (NB - 1) * P
            sp.wait_ge(xo_ready, GROUPS - 1)
            for t, s in ((xs, x), (sk, skip_dram)):
                sp.dma_start(t[:, 0, 0:REST - 1, :], s[r0:r1, :].rearrange("(u p) d -> p u d", p=P)).then_inc(loaded[0], 16)
                sp.dma_start(t[0:N - r1, 0, REST - 1, :], s[r1:N, :]).then_inc(loaded[0], 16)
            store(GROUPS - 1, 1)
            sp.wait_ge(res_ready, GROUPS + 1)
            sp.dma_start(out[r0:r1, :].rearrange("(u p) d -> p u d", p=P), res[:, 0, 0:REST - 1, :]).then_inc(out_stored[0], 16)
            sp.dma_start(out[r1:N, :], res[0:N - r1, 0, REST - 1, :]).then_inc(out_stored[0], 16)
            sp.wait_ge(out_stored[0], 16 * (GROUPS // 2) + 32)
            sp.wait_ge(out_stored[1], 16 * (GROUPS // 2))

        @block.vector
        def _(dve):
            V = nc.vector

            def head(it, k, w, loads):
                g = 2 * it + k
                rows = acc[:, bass.ds(g * WID, w), :].rearrange("p u (h c) -> p u h c", c=CW)
                V.tensor_scalar(den[:, k, 0:w, :], rows[:, :, :, C], EPS_SUM, None, ALU.add).then_inc(den_add, 1)
                dve.wait_ge(den_add, g + 1)
                V.reciprocal(den[:, k, 0:w, :], den[:, k, 0:w, :]).then_inc(den_inv, 1)
                dve.wait_ge(den_inv, g + 1)
                wait(dve, ot_ps, g - 1)
                wait(dve, xo_ready, g - 1)
                ov = o[:, k, 0:w, :].rearrange("p u (h c) -> p u h c", h=H)
                V.tensor_tensor(ov, rows[:, :, :, 0:C], den[:, k, 0:w, :].unsqueeze(3).broadcast_to([P, w, H, C]), ALU.mult).then_inc(normed, 1)
                dve.wait_ge(normed, g + 1)
                dve.wait_ge(loaded[k], loads)
                V.tensor_tensor(o[:, k, 0:w, :], o[:, k, 0:w, :], sk[:, k, 0:w, :], ALU.add).then_inc(out_ready, 1)
                wait(dve, out_stored[k], 16 * it)
                dve.wait_ge(out_ready, g + 1)
                V.tensor_tensor(res[:, k, 0:w, :], o[:, k, 0:w, :], xs[:, k, 0:w, :], ALU.add).then_inc(xo_ready, 1)

            def tail(g, k, w):
                dve.wait_ge(y_ps, g + 1)
                dve.wait_ge(xo_ready, g + 1)
                V.tensor_tensor(res[:, k, 0:w, :].rearrange("p u d -> p (u d)"), res[:, k, 0:w, :].rearrange("p u d -> p (u d)"),
                                p_3[:, 0:w * D], ALU.add).then_inc(res_ready, 1)

            def body(it, k, w=WID):
                g = 2 * it + k
                head(it, k, w, 32 * (it + 1) + 32 * (w < WID))
                if not isinstance(g, int) or g >= 1:
                    tail(g - 1, 1 - k, WID)

            body(0, 0)
            body(0, 1)
            with dve.Fori(1, GROUPS // 2) as it:
                body(it, 0)
                body(it, 1)
            body(GROUPS // 2, 0, REST)
            tail(GROUPS, 0, REST)

        @block.scalar
        def _(act):
            S = nc.scalar

            def step(g, w=WID):
                m = w * P
                act.wait_ge(ot_ps, g + 1)
                S.activation(ot[:, 0:m], p_o[:, 0:m], ACT.Copy).then_inc(ot_sb, 1)
                act.wait_ge(h1_ps, g + 1)
                S.activation(h1[:, 0:m], p_1[:, 0:m], ACT.Gelu_apprx_tanh, bias=b1s[:, 0:1]).then_inc(h1_sb, 1)
                act.wait_ge(h2_ps, g + 1)
                wait(act, y_ps, g)
                S.activation(h2[:, 0:m], p_2[:, 0:m], ACT.Gelu_apprx_tanh, bias=b2s[:, 0:1]).then_inc(h2_sb, 1)

            act.wait_ge(w_in3, 64)
            step(0)
            with act.Fori(1, GROUPS) as g:
                step(g)
            step(GROUPS, REST)

        @block.tensor
        def _(pe):
            T = nc.tensor

            def transposes(g, k, w=WID):
                pe.wait_ge(out_ready, g + 1)
                wait(pe, ot_sb, g)
                for u in range(w):
                    last = T.transpose(p_o[:, u * P:(u + 1) * P], o[:, k, u, :], ident[:])
                last.then_inc(ot_ps, 1)

            def mlp(g, k, w=WID):
                m = w * P
                pe.wait_ge(ot_sb, g + 1)
                T.matmul(p_1[:, 0:m], w1s[:], ot[:, 0:m], start=True, stop=True).then_inc(h1_ps, 1)
                pe.wait_ge(h1_sb, g + 1)
                T.matmul(p_2[:, 0:m], w2s[:], h1[:, 0:m], start=True, stop=True).then_inc(h2_ps, 1)
                pe.wait_ge(h2_sb, g + 1)
                wait(pe, res_ready, g)
                for u in range(w):
                    last = T.transpose(p_3[:, u * P:(u + 1) * P], h2[:, u * P:(u + 1) * P], ident[:])
                last.then_inc(y_ps, 1)

            pe.wait_ge(w_in3, 64)
            for k in range(2):
                transposes(k, k)
                mlp(k, k)
            with pe.Fori(1, GROUPS // 2) as it:
                for k in range(2):
                    transposes(2 * it + k, k)
                    mlp(2 * it + k, k)
            transposes(GROUPS, 0, REST)
            mlp(GROUPS, 0, REST)


def graph_transformer(nc, x, src, dst, attr, wq, bq, wk, bk, wv, bv, we, wskip, bskip, w1, b1, w2, b2, out):
    def scratch(name, shape, dt=F32):
        return nc.dram_tensor(name, shape, dt, kind="Internal").ap()

    dram = (scratch("kv_rows", (N, 2 * D)), scratch("skip_rows", (N, D)),
            scratch("dst_tiles", (NI, P), I32), scratch("src_tiles", (NI, P), I32),
            scratch("tags", (NI * P + 2,)), scratch("penalties", (NI, P + 1)),
            scratch("carry_penalties", (NBATCH, 2, H * CW)), scratch("item_edges", (NBATCH, P, 2 * BI), I32),
            scratch("item_blocks", (NI,), I32), scratch("attr_end", (NTAIL * P, A)))
    with ExitStack() as ctx:
        acc = ctx.enter_context(nc.sbuf_tensor("acc", [P, NB, H * CW], F32))
        ident = ctx.enter_context(nc.sbuf_tensor("ident", [P, P], F32))
        with ExitStack() as inner:
            qt = inner.enter_context(nc.sbuf_tensor("qt", [P, NB, D], F32))
            brow = inner.enter_context(nc.sbuf_tensor("brow", [1, NI], I32))
            index_and_nodes(nc, x, src, dst, attr, wq, bq, wk, bk, wv, bv, wskip, bskip, dram, qt, acc, ident, brow)
            edges(nc, attr, we, dram, qt, acc, ident, brow)
        output(nc, x, w1, b1, w2, b2, out, dram, acc, ident)


_INS = ['x', 'src', 'dst', 'edge_attr_32', 'L0_gnn_Wq', 'L0_gnn_bq', 'L0_gnn_Wk', 'L0_gnn_bk', 'L0_gnn_Wv', 'L0_gnn_bv',
        'L0_gnn_We', 'L0_gnn_Wskip', 'L0_gnn_bskip', 'L0_gnn_W1', 'L0_gnn_b1', 'L0_gnn_W2', 'L0_gnn_b2']
_OUTS = [((12500, 128), 'float32')]


def kernel(**inputs):
    import numpy as _np
    import concourse.bacc as _bacc
    from concourse import mybir as _mybir
    from concourse.bass_utils import run_bass_kernel_spmd as _run

    nc = _bacc.Bacc("TRN2", target_bir_lowering=False, num_devices=1)
    arrays, args = {}, []
    for name in _INS:
        a = _np.ascontiguousarray(inputs[name])
        arrays[f"in_{name}_dram"] = a
        args.append(nc.dram_tensor(f"in_{name}_dram", a.shape, _mybir.dt.from_np(a.dtype), kind="ExternalInput").ap())
    for i, (shape, dtype) in enumerate(_OUTS):
        dt = _mybir.dt.from_np(_np.dtype(dtype))
        args.append(nc.dram_tensor(f"out_{i}_dram", shape, dt, kind="ExternalOutput").ap())
    graph_transformer(nc, *args)
    r = _run(nc, [arrays], core_ids=[0])
    got = tuple(r.results[0][f"out_{i}_dram"] for i in range(len(_OUTS)))
    return got[0]
```

```python
from contextlib import ExitStack

import concourse.bass as bass
from concourse import mybir

F32 = mybir.dt.float32
I32 = mybir.dt.int32
ALU = mybir.AluOpType
ACT = mybir.ActivationFunctionType
AX = mybir.AxisListType
EngineType = mybir.EngineType

P = 128
N, E, D, H, A = 12500, 200000, 128, 4, 32
C = D // H
CW = C + 1
NB = -(-N // P)
NT = -(-E // P)
GI = 4
BI = 32
GB = BI // GI
NBATCH = -(-(NT + NB - 1) // BI)
NI = NBATCH * BI
NC = NI // P
NG = NI // GI
SLOTS = 4
RING = 2 * GB
LAG = GB + GB // 2
PAD = 1 << 14
BIG = 1.0e30
SCALE = float(C) ** -0.5
EPS_LN, EPS_SUM = 1e-5, 1e-16
TAIL0 = (NBATCH - 4) * BI - NB
NTAIL = NI - (NBATCH - 4) * BI + NB
CB = 7
NCH = NB // CB


def wait(engine, semaphore, value):
    if not isinstance(value, int) or value > 0:
        engine.wait_ge(semaphore, value)


def wait_apart(engine, reached, *waits):
    for semaphore, value in waits:
        if not isinstance(value, int):
            engine.to_reg(value)
    engine.wait_ge(reached, 1)
    for semaphore, value in waits:
        wait(engine, semaphore, value)


def live(group):
    return not isinstance(group, int) or 0 <= group < NG


def index_and_nodes(nc, x, src, dst, attr, wq, bq, wk, bk, wv, bv, wskip, bskip, dram, qt, acc, ident, brow):
    kv_dram, skip_dram, dst_dram, src_dram, tag_dram, pen_dram, cp_dram, erec_dram, brow_dram, tail_dram = dram
    NQ = 4 * D
    FULL = (NT // P) * P
    REST = E // P - FULL
    LAST = E - (FULL + REST) * P

    with ExitStack() as ctx:
        def sb(name, shape, dt=F32):
            return ctx.enter_context(nc.sbuf_tensor(name, shape, dt))

        def sem(name):
            return ctx.enter_context(nc.semaphore(name))

        flat, used = acc[:].rearrange("p b f -> p (b f)"), [0]

        def part(shape):
            at, size = used[0], shape[0] * shape[1]
            used[0] += size
            return flat[:, at:at + size].rearrange("p (a b) -> p a b", a=shape[0])

        xs = sb("xs", [P, 2, CB, D])
        w4 = sb("w4", [P, NQ])
        bias4 = sb("bias4", [P, NQ])
        stats = sb("stats", [P, 2, CB, 6])
        mv = sb("mv", [P, 2, CB, 2])
        std = sb("std", [P, 2, CB])
        rstd = sb("rstd", [P, 2, CB])
        eps = sb("eps", [P, 1])
        xn = sb("xn", [P, 2, D])
        ht = sb("ht", [P, 2, P])
        kvs = sb("kvs", [P, 2, CB, 2 * D])
        sks = sb("sks", [P, 2, CB, D])

        dt_i = sb("dt_i", [P, NC, P], I32)
        st_i = sb("st_i", [P, NC, P], I32)
        di_i = sb("di_i", [P, NC, P], I32)
        si_i = sb("si_i", [P, NC, P], I32)
        di = part([NC, P])
        si = part([NC, P])
        ndl = sb("ndl", [P, NC, P])
        tag = part([NC, P])
        tagp = part([NC, P])
        tagn = part([NC, P])
        lastd = sb("lastd", [P, NC])
        kint = sb("kint", [P, NB], I32)
        kf = sb("kf", [P, NB])
        k128 = sb("k128", [P, NB])
        iint = sb("iint", [P, NC], I32)
        ifl = sb("ifl", [P, NC])
        cmp1 = part([NB, NC])
        cmp2 = part([NC, NB])
        cnt = sb("cnt", [P, NB])
        start = sb("start", [P, NB])
        ones = sb("ones", [P, P])
        bsum = sb("bsum", [P, NC])
        bf = sb("bf", [P, NC])
        b128 = sb("b128", [P, NC])
        tf = sb("tf", [P, NC])
        ti = sb("ti", [P, NC], I32)
        cp = sb("cp", [P, 2, NC])
        cpx = sb("cpx", [NC, 2, 4, H, CW])
        bti = sb("bti", [NC, P], I32)
        cap = sb("cap", [1, 1])
        erec = sb("erec", [P, NC, 4, 2 * BI], I32)

        with ExitStack() as pctx:
            def pb(name, shape):
                return pctx.enter_context(nc.psum_tensor(name, shape, F32))

            p_t = [pb(f"p_t{i}", [P, 512]) for i in range(2)]
            p_q = [pb(f"p_q{i}", [P, NQ]) for i in range(2)]
            p_i = pb("p_i", [P, 512])

            x_in = [sem(f"x_in{i}") for i in range(2)]
            w_in = sem("w_in")
            stored = [sem(f"stored{i}") for i in range(2)]
            d_in, s_in = sem("d_in"), sem("s_in")
            scratch_out = sem("scratch_out")
            di_in, si_in = sem("di_in"), sem("si_in")
            tag_out, tagp_in, pen_out, idx_out, brow_out, brow_in, tail_out = (
                sem(n) for n in ("tag_out", "tagp_in", "pen_out", "idx_out", "brow_out", "brow_in", "tail_out"))
            pads, consts, iotas, caps = sem("pads"), sem("consts"), sem("iotas"), sem("caps")
            chain = sem("index_chain")
            cnt_ready, count_ps, ti_ready, tag_ready, pen_ready, tagn_pen, cp_ready = (
                sem(n) for n in ("cnt_ready", "count_ps", "ti_ready", "tag_ready", "pen_ready", "tagn_pen", "cp_ready"))
            si_f, tr_ps, tr_sb, small_ps, small_sb = (sem(n) for n in ("si_f", "tr_ps", "tr_sb", "small_ps", "small_sb"))
            stats_done, aggr_done, std_done, rstd_done = (sem(n) for n in ("stats_done", "aggr_done", "std_done", "rstd_done"))
            xn_ready, xt_ps, ht_ready, qkvs_ps, qkvs_out = (sem(n) for n in ("xn_ready", "xt_ps", "ht_ready", "qkvs_ps", "qkvs_out"))
            block = pctx.enter_context(nc.Block())

            @block.sync
            def _(sp):
                sp.dma_start(dt_i[:, 0:NC - 1, :], dst[0:FULL * P].rearrange("(c p e) -> p c e", p=P, e=P)).then_inc(d_in, 16)
                sp.dma_start(st_i[:, 0:NC - 1, :], src[0:FULL * P].rearrange("(c p e) -> p c e", p=P, e=P)).then_inc(s_in, 16)
                for i, w in enumerate((wk, wv, wq, wskip)):
                    sp.dma_start(w4[:, i * D:(i + 1) * D], w).then_inc(w_in, 16)
                for i, b in enumerate((bk, bv, bq, bskip)):
                    sp.dma_start(bias4[:, i * D:(i + 1) * D],
                                 b.rearrange("(a c) -> a c", a=1).broadcast_to([P, D])).then_inc(w_in, 16)

                def load_x(c, ch):
                    wait(sp, xn_ready, (c - 1) * CB)
                    sp.dma_start(xs[:, ch, :, :], x[bass.ds(c * (CB * P), CB * P), :].rearrange("(u p) d -> p u d", p=P)
                                 ).then_inc(x_in[ch], 16)

                def store_nodes(c, ch):
                    sp.wait_ge(qkvs_out, (c + 1) * CB)
                    rows = bass.ds(c * (CB * P), CB * P)
                    sp.dma_start(kv_dram[rows, :].rearrange("(u p) d -> p u d", p=P), kvs[:, ch, :, :]).then_inc(stored[ch], 16)
                    sp.dma_start(skip_dram[rows, :].rearrange("(u p) d -> p u d", p=P), sks[:, ch, :, :]).then_inc(stored[ch], 16)

                load_x(0, 0)
                load_x(1, 1)
                sp.wait_ge(pads, 1)
                sp.dma_start(dt_i[0:REST, NC - 1, :], dst[FULL * P:(FULL + REST) * P].rearrange("(p e) -> p e", e=P)).then_inc(d_in, 16)
                sp.dma_start(dt_i[REST:REST + 1, NC - 1, 0:LAST], dst[(FULL + REST) * P:E].rearrange("(p e) -> p e", p=1)).then_inc(d_in, 16)
                sp.wait_ge(pads, 2)
                sp.dma_start(st_i[0:REST, NC - 1, :], src[FULL * P:(FULL + REST) * P].rearrange("(p e) -> p e", e=P)).then_inc(s_in, 16)
                sp.dma_start(st_i[REST:REST + 1, NC - 1, 0:LAST], src[(FULL + REST) * P:E].rearrange("(p e) -> p e", p=1)).then_inc(s_in, 16)
                sp.wait_ge(d_in, 48)
                sp.dma_start(dst_dram.rearrange("(c p) e -> p c e", p=P), dt_i[:]).then_inc(scratch_out, 16)
                sp.wait_ge(s_in, 48)
                sp.dma_start(src_dram.rearrange("(c p) e -> p c e", p=P), st_i[:]).then_inc(scratch_out, 16)
                rows = E - TAIL0 * P
                sp.dma_start(tail_dram[0:rows, :], attr[TAIL0 * P:E, :]).then_inc(tail_out, 16)
                sp.dma_start(tail_dram[rows:NTAIL * P, :], attr[0:NTAIL * P - rows, :]).then_inc(tail_out, 16)

                with sp.Fori(0, NCH // 2 - 2) as it:
                    for ch in range(2):
                        load_x(2 * it + 2 + ch, ch)
                        store_nodes(2 * it + ch, ch)
                load_x(NCH - 2, 0)
                store_nodes(NCH - 4, 0)
                r0, r1 = (NB - CB) * P, (NB - 1) * P
                sp.wait_ge(xn_ready, (NCH - 2) * CB)
                sp.dma_start(xs[:, 1, 0:CB - 1, :], x[r0:r1, :].rearrange("(u p) d -> p u d", p=P)).then_inc(x_in[1], 16)
                sp.dma_start(xs[0:N - r1, 1, CB - 1, :], x[r1:N, :]).then_inc(x_in[1], 16)
                store_nodes(NCH - 3, 1)
                store_nodes(NCH - 2, 0)
                sp.wait_ge(qkvs_out, NB)
                for dram_t, s in ((kv_dram, kvs), (skip_dram, sks)):
                    sp.dma_start(dram_t[r0:r1, :].rearrange("(u p) d -> p u d", p=P), s[:, 1, 0:CB - 1, :]).then_inc(stored[1], 16)
                    sp.dma_start(dram_t[r1:N, :], s[0:N - r1, 1, CB - 1, :]).then_inc(stored[1], 16)

                sp.wait_ge(tag_ready, 1)
                sp.wait_ge(caps, 1)
                sp.dma_start(tag_dram[1:1 + NI * P].rearrange("(c p e) -> p c e", p=P, e=P), tag).then_inc(tag_out, 16)
                sp.dma_start(tag_dram[0:1].rearrange("(a e) -> a e", a=1), cap[0:1, 0:1]).then_inc(tag_out, 16)
                sp.dma_start(tag_dram[1 + NI * P:2 + NI * P].rearrange("(a e) -> a e", a=1), cap[0:1, 0:1]).then_inc(tag_out, 16)
                sp.wait_ge(tag_out, 48)
                sp.dma_start(tagp, tag_dram[0:NI * P].rearrange("(c p e) -> p c e", p=P, e=P)).then_inc(tagp_in, 16)
                sp.dma_start(tagn, tag_dram[2:2 + NI * P].rearrange("(c p e) -> p c e", p=P, e=P)).then_inc(tagp_in, 16)
                sp.wait_ge(pen_ready, 1)
                sp.dma_start(pen_dram[:, 0:P].rearrange("(c p) e -> p c e", p=P), tagp).then_inc(pen_out, 16)
                sp.wait_ge(tagn_pen, 1)
                sp.dma_start(pen_dram[:, P:P + 1].rearrange("(c p) e -> p c e", p=P), tagn[:, :, P - 1:P],
                             allow_slow_non_contiguous=True).then_inc(pen_out, 16)
                sp.wait_ge(small_sb, 1)
                sp.dma_start(brow_dram.rearrange("(c i) -> c i", c=NC), bti[:]).then_inc(brow_out, 16)
                sp.wait_ge(brow_out, 16)
                sp.dma_start(brow[:], brow_dram.rearrange("(a i) -> a i", a=1)).then_inc(brow_in, 16)
                sp.wait_ge(small_sb, 3)
                for d in range(2):
                    sp.dma_start(cp_dram[:, d, :].rearrange("(c q) f -> c q f", q=4),
                                 cpx[:, d, :, :, :].rearrange("c q h t -> c q (h t)")).then_inc(idx_out, 16)
                sp.wait_ge(tr_sb, 2 * NC)
                sp.dma_start(erec_dram.rearrange("j e f -> e j f"), erec[:].rearrange("e c q f -> e (c q) f")).then_inc(idx_out, 16)
                sp.wait_ge(idx_out, 48)
                sp.wait_ge(pen_out, 32)
                sp.wait_ge(brow_in, 16)
                sp.wait_ge(tail_out, 32)
                sp.wait_ge(stored[0], 32 * (NCH // 2))
                sp.wait_ge(stored[1], 32 * (NCH // 2 - 1) + 64)

            @block.gpsimd
            def _(pool):
                nc.gpsimd.memset(dt_i[:, NC - 1, :], PAD).then_inc(pads, 1)
                nc.gpsimd.memset(st_i[:, NC - 1, :], 0).then_inc(pads, 1)
                nc.gpsimd.memset(ones[:], 1.0).then_inc(consts, 1)
                nc.gpsimd.memset(ident[:], 0.0).then_inc(consts, 1)
                pool.wait_ge(consts, 2)
                nc.gpsimd.affine_select(out=ident[:], in_=ident[:], compare_op=ALU.not_equal, fill=1.0, base=0,
                                        pattern=[[-1, P]], channel_multiplier=1).then_inc(consts, 1)
                nc.gpsimd.iota(kint[:], pattern=[[1, NB]], base=0, channel_multiplier=0).then_inc(iotas, 1)
                nc.gpsimd.iota(iint[:], pattern=[[P, NC]], base=0, channel_multiplier=1).then_inc(iotas, 1)
                nc.gpsimd.memset(cap[:, 0:1], -1.0).then_inc(caps, 1)
                nc.gpsimd.memset(cpx[:], -BIG).then_inc(caps, 1)
                pool.wait_ge(ti_ready, 1)
                pool.wait_ge(scratch_out, 32)
                for c in range(NC):
                    at = bass.IndirectOffsetOnAxis(ap=ti[:, c:c + 1], axis=0)
                    nc.gpsimd.indirect_dma_start(out=di_i[:, c, :], out_offset=None, in_=dst_dram, in_offset=at).then_inc(di_in, 16)
                for c in range(NC):
                    at = bass.IndirectOffsetOnAxis(ap=ti[:, c:c + 1], axis=0)
                    nc.gpsimd.indirect_dma_start(out=si_i[:, c, :], out_offset=None, in_=src_dram, in_offset=at).then_inc(si_in, 16)

            @block.vector
            def _(dve):
                V = nc.vector
                done = [0]

                def link(ins):
                    done[0] += 1
                    ins.then_inc(chain, 1)
                    dve.wait_ge(chain, done[0])

                V.memset(eps[:], EPS_LN)
                dve.wait_ge(iotas, 2)
                V.tensor_copy(kf[:], kint[:])
                link(V.tensor_copy(ifl[:], iint[:]))
                dve.wait_ge(d_in, 48)
                V.tensor_copy(lastd[:], dt_i[:, :, P - 1])
                link(V.tensor_scalar(k128[:], kf[:], float(P), None, ALU.mult))
                link(V.tensor_tensor(cmp1, lastd[:].unsqueeze(1).broadcast_to([P, NB, NC]),
                                     k128[:].unsqueeze(2).broadcast_to([P, NB, NC]), ALU.is_lt))
                V.tensor_reduce(cnt[:], cmp1, axis=AX.X, op=ALU.add).then_inc(cnt_ready, 1)
                dve.wait_ge(count_ps, 1)
                link(V.tensor_tensor(start[:], p_i[:, 0:NB], kf[:], ALU.add))
                link(V.tensor_tensor(cmp2, start[:].unsqueeze(1).broadcast_to([P, NC, NB]),
                                     ifl[:].unsqueeze(2).broadcast_to([P, NC, NB]), ALU.is_le))
                link(V.tensor_reduce(bsum[:], cmp2, axis=AX.X, op=ALU.add))
                link(V.tensor_scalar(bf[:], bsum[:], -1.0, None, ALU.add))
                link(V.tensor_tensor(tf[:], ifl[:], bf[:], ALU.subtract))
                V.tensor_scalar(b128[:], bf[:], float(P), None, ALU.mult)
                V.tensor_copy(ti[:], tf[:]).then_inc(ti_ready, 1)

                def add_bias(it, k):
                    n = 2 * CB * it + k
                    ch, v = k // CB, k % CB
                    if v == 0:
                        wait(dve, stored[ch], 32 * it)
                    dve.wait_ge(qkvs_ps, n + 1)
                    pq = p_q[k % 2]
                    V.tensor_tensor(kvs[:, ch, v, :], pq[:, 0:2 * D], bias4[:, 0:2 * D], ALU.add)
                    V.tensor_tensor(qt[:, bass.ds(n, 1), :].rearrange("p a d -> p (a d)"), pq[:, 2 * D:3 * D], bias4[:, 2 * D:3 * D], ALU.add)
                    V.tensor_tensor(sks[:, ch, v, :], pq[:, 3 * D:NQ], bias4[:, 3 * D:NQ], ALU.add).then_inc(qkvs_out, 1)

                def chunk(it, ch, more, last=False):
                    c = 2 * it + ch
                    nx = 1 - ch
                    for u in range(CB):
                        n = c * CB + u
                        k = ch * CB + u
                        wait(dve, xt_ps, n - 1)
                        if u == 0:
                            dve.wait_ge(rstd_done, c + 1)
                        V.tensor_scalar(xn[:, k % 2, :], xs[:, ch, u, :],
                                        mv[:, ch, u, 0:1], rstd[:, ch, u:u + 1], ALU.subtract, ALU.mult).then_inc(xn_ready, 1)
                        if more:
                            if u == 0:
                                dve.wait_ge(x_in[nx], 16 * (it + 1 + ch) + 16 * (last and ch == 0))
                            V.bn_stats(stats[:, nx, u, :], xs[:, nx, u, :]).then_inc(stats_done, 1)
                        if k >= 2:
                            add_bias(it, k - 2)
                        elif not isinstance(it, int) or it > 0:
                            add_bias(it - 1, k - 2 + 2 * CB)
                        if more:
                            wait_apart(dve, w_in, (stats_done, (c + 1) * CB + u + 1))
                            V.bn_aggr(mv[:, nx, u, :], stats[:, nx, u, :]).then_inc(aggr_done, 1)
                    if more:
                        dve.wait_ge(std_done, c + 2)
                        V.reciprocal(rstd[:, nx, :], std[:, nx, :]).then_inc(rstd_done, 1)

                dve.wait_ge(x_in[0], 16)
                for u in range(CB):
                    V.bn_stats(stats[:, 0, u, :], xs[:, 0, u, :]).then_inc(stats_done, 1)
                for u in range(CB):
                    dve.wait_ge(stats_done, u + 1)
                    V.bn_aggr(mv[:, 0, u, :], stats[:, 0, u, :]).then_inc(aggr_done, 1)
                dve.wait_ge(std_done, 1)
                V.reciprocal(rstd[:, 0, :], std[:, 0, :]).then_inc(rstd_done, 1)
                dve.wait_ge(w_in, 128)
                chunk(0, 0, True)
                chunk(0, 1, True)
                with dve.Fori(1, NCH // 2 - 1) as it:
                    chunk(it, 0, True)
                    chunk(it, 1, True)
                chunk(NCH // 2 - 1, 0, True, last=True)
                chunk(NCH // 2 - 1, 1, False)
                add_bias(NCH // 2 - 1, 2 * CB - 2)
                add_bias(NCH // 2 - 1, 2 * CB - 1)

                dve.wait_ge(di_in, 16 * NC)
                link(V.tensor_copy(di, di_i[:]))
                bcast = b128[:].unsqueeze(2).broadcast_to([P, NC, P])
                V.tensor_scalar(tag, di, float(P), None, ALU.mult).then_inc(chain, 1)
                done[0] += 1
                V.tensor_tensor(ndl[:], bcast, di, ALU.subtract)
                dve.wait_ge(chain, done[0])
                V.tensor_tensor(tag, tag, bf[:].unsqueeze(2).broadcast_to([P, NC, P]), ALU.add).then_inc(tag_ready, 1)
                dve.wait_ge(si_in, 16 * NC)
                V.tensor_copy(si, si_i[:]).then_inc(si_f, 1)
                for n in range(2 * NC):
                    c, which = n // 2, n % 2
                    dve.wait_ge(tr_ps, n + 1)
                    pv = p_t[which][:, 0:P].rearrange("e (q t) -> e q t", q=4)
                    if which == 0:
                        V.tensor_copy(erec[:, c, :, 0:BI], pv).then_inc(tr_sb, 1)
                    else:
                        V.tensor_copy(erec[:, c, :, BI:2 * BI].bitcast(F32), pv).then_inc(tr_sb, 1)
                dve.wait_ge(tagp_in, 32)
                link(V.tensor_tensor(tagp, tag, tagp, ALU.not_equal))
                link(V.tensor_tensor(tagn, tag, tagn, ALU.not_equal))
                V.tensor_scalar(tagp, tagp, -BIG, None, ALU.mult).then_inc(pen_ready, 1)
                V.tensor_scalar(tagn, tagn, -BIG, None, ALU.mult).then_inc(tagn_pen, 1)
                dve.wait_ge(tagn_pen, 1)
                dve.wait_ge(pen_ready, 1)
                V.tensor_reduce(cp[:, 0, :], tagp, axis=AX.X, op=ALU.add).then_inc(cp_ready, 1)
                V.tensor_reduce(cp[:, 1, :], tagn, axis=AX.X, op=ALU.add).then_inc(cp_ready, 1)
                dve.wait_ge(small_ps, 1)
                V.tensor_copy(bti[:], p_i[0:NC, 0:P]).then_inc(small_sb, 1)
                dve.wait_ge(caps, 2)
                for d in range(2):
                    dve.wait_ge(small_ps, 2 + d)
                    V.tensor_copy(cpx[:, d, :, :, (1 - d):(1 - d) + BI],
                                  p_i[0:NC, P * (1 + d):P * (2 + d)].rearrange("c (q t) -> c q t", q=4).unsqueeze(2)
                                  .broadcast_to([NC, 4, H, BI])).then_inc(small_sb, 1)

            @block.scalar
            def _(act):
                S = nc.scalar

                def chunk_std(c, ch):
                    act.wait_ge(aggr_done, (c + 1) * CB)
                    S.activation(std[:, ch, :], mv[:, ch, :, 1], ACT.Sqrt, bias=eps[:, 0:1]).then_inc(std_done, 1)

                def blocks(c, ch):
                    for u in range(CB):
                        n = c * CB + u
                        k = (ch * CB + u)
                        act.wait_ge(xt_ps, n + 1)
                        wait(act, qkvs_ps, n - 1)
                        S.activation(ht[:, k % 2, :], p_t[k % 2][:, 0:P], ACT.Relu).then_inc(ht_ready, 1)

                chunk_std(0, 0)
                for ch in range(2):
                    blocks(ch, ch)
                    chunk_std(ch + 1, 1 - ch)
                with act.Fori(1, NCH // 2 - 1) as it:
                    for ch in range(2):
                        blocks(2 * it + ch, ch)
                        chunk_std(2 * it + ch + 1, 1 - ch)
                blocks(NCH - 2, 0)
                chunk_std(NCH - 1, 1)
                blocks(NCH - 1, 1)

            @block.tensor
            def _(pe):
                T = nc.tensor
                pe.wait_ge(consts, 3)
                pe.wait_ge(cnt_ready, 1)
                T.matmul(p_i[:, 0:NB], ones[:], cnt[:], start=True, stop=True).then_inc(count_ps, 1)
                pe.wait_ge(w_in, 128)

                def transpose(n, k):
                    pe.wait_ge(xn_ready, n + 1)
                    wait(pe, ht_ready, n - 1)
                    T.transpose(p_t[k % 2][:, 0:P], xn[:, k % 2, :], ident[:]).then_inc(xt_ps, 1)

                def product(n, k):
                    pe.wait_ge(ht_ready, n + 1)
                    wait(pe, qkvs_out, n - 1)
                    T.matmul(p_q[k % 2][:], ht[:, k % 2, :], w4[:], start=True, stop=True).then_inc(qkvs_ps, 1)

                def pair(it):
                    for k in range(2 * CB):
                        transpose(2 * CB * it + k, k)
                        if k >= 1:
                            product(2 * CB * it + k - 1, k - 1)
                    product(2 * CB * it + 2 * CB - 1, 2 * CB - 1)

                pair(0)
                with pe.Fori(1, NCH // 2) as it:
                    pair(it)
                pe.wait_ge(si_f, 1)
                for n in range(2 * NC):
                    wait(pe, tr_sb, n - 1)
                    T.transpose(p_t[n % 2][:, 0:P], (si if n % 2 == 0 else ndl)[:, n // 2, :], ident[:]).then_inc(tr_ps, 1)
                T.transpose(p_i[0:NC, 0:P], bf[:], ident[:]).then_inc(small_ps, 1)
                pe.wait_ge(cp_ready, 2)
                for d in range(2):
                    pe.wait_ge(small_sb, 1 + d)
                    T.transpose(p_i[0:NC, P * (1 + d):P * (2 + d)], cp[:, d, :], ident[:]).then_inc(small_ps, 1)


def edges(nc, attr, we, dram, qt, acc, ident, brow):
    kv_dram, skip_dram, dst_dram, src_dram, tag_dram, pen_dram, cp_dram, erec_dram, brow_dram, tail_dram = dram
    UNR = 2 * GB
    TURNS = NG // UNR
    PENS = H + 1
    STEPS_LEFT = LAG + 1

    with ExitStack() as ctx:
        def sb(name, shape, dt=F32):
            return ctx.enter_context(nc.sbuf_tensor(name, shape, dt))

        def pb(name, shape):
            return ctx.enter_context(nc.psum_tensor(name, shape, F32))

        def sem(name):
            return ctx.enter_context(nc.semaphore(name))

        val = sb("val", [P, RING, GI, H, CW])
        onehot = sb("onehot", [P, RING, GI, P])
        kvr = sb("kvr", [P, SLOTS, GI, 2 * D])
        araw = sb("araw", [P, SLOTS, GI, A])
        at = sb("at", [P, P])
        st = sb("st", [P, GI, P])
        we4 = sb("we4", [P, GI, D])
        wv = sb("wv", [P, 2, GI, H * CW])
        alpha = sb("alpha", [P, 2, H, BI])
        ex = sb("ex", [P, 2, H, BI])
        erec = sb("erec2", [P, 2, 2 * BI], I32)
        pen = sb("pen", [P, 2, P + 1])
        fwd = sb("fwd", [P, P])
        bwd = sb("bwd", [P, P])
        cin = sb("cin", [P, 2])
        fac = sb("fac", [P, H])
        iota_f = sb("iota_f", [P, P])
        iota_i = fwd[:, :].bitcast(I32)
        sel4 = sb("sel4", [P, H])
        one = sb("one", [1, 1])
        cpr = sb("cpr", [1, 2, 2, H * CW])
        zf = sb("zf", [1, H, CW])
        rf = sb("rf", [1, H, CW])
        zb = sb("zb", [1, H, CW])
        dm = sb("dm", [1, 2, H])

        p_e = pb("p_e", [P, 512])
        p_qd = pb("p_qd", [P, 512])
        p_st = pb("p_st", [P, 512])
        p_ag = [pb(f"p_ag{i}", [P, 512]) for i in range(2)]
        p_at = pb("p_at", [P, 512])
        p_al = pb("p_al", [P, 512])
        p_sm = pb("p_sm", [P, 512])
        p_row, p_col, p_m, p_f = p_sm[0:1, 0:P], p_sm[:, P:P + 1], p_sm[0:1, 132:132 + H], p_sm[:, 140:140 + H]
        p_ex = p_al[:, 256:256 + P]

        kv_in = [sem(f"kv_in{i}") for i in range(SLOTS)]
        attr_in = [sem(f"attr_in{i}") for i in range(SLOTS)]
        erec_in = [sem(f"erec_in{i}") for i in range(2)]
        pen_in = [sem(f"pen_in{i}") for i in range(2)]
        we_in, setup = sem("we_in"), sem("setup")
        at_ps, at_sb, st_ps, st_sb, sq_done, onehot_done = (sem(n) for n in ("at_ps", "at_sb", "st_ps", "st_sb", "sq_done", "onehot_done"))
        e_ps, q_ps, k_done, v_done, prod_done, alpha_done = (sem(n) for n in ("e_ps", "q_ps", "k_done", "v_done", "prod_done", "alpha_done"))
        wv_done, agg_ps, acc_done, scaled = (sem(n) for n in ("wv_done", "agg_ps", "acc_done", "scaled"))
        al_ps, last_f, row_f, carry_f, z_f, run_f, col_f, cin_f, fwd_done = (
            sem(n) for n in ("al_ps", "last_f", "row_f", "carry_f", "z_f", "run_f", "col_f", "cin_f", "fwd_done"))
        first_b, row_b, z_b, run_b, col_b, cin_b, max_done = (
            sem(n) for n in ("first_b", "row_b", "z_b", "run_b", "col_b", "cin_b", "max_done"))
        diff_done, ext_done, ex_ps, ex_done, m_ps, dm_sub, dm_done, f_ps, f_done = (
            sem(n) for n in ("diff_done", "ext_done", "ex_ps", "ex_done", "m_ps", "dm_sub", "dm_done", "f_ps", "f_done"))
        block = ctx.enter_context(nc.Block())

        def blocks_of(engine, n):
            return nc.values_load_multi_w_load_instructions(
                brow[0:1, bass.ds(GI * n, GI)], engines=[engine], min_val=0, max_val=NB - 1,
                skip_runtime_bounds_check_because="b[i] counts blocks started, out of NB")[1]

        def behind(turn, s):
            j = 2 * turn + s // GB - 1
            return (j, (s // GB + 1) % 2) if not isinstance(j, int) or 0 <= j < NBATCH else (None, None)

        @block.sync
        def _(sp):
            sp.wait_ge(setup, 1)
            for i in range(GI):
                sp.dma_start(we4[A * i:A * (i + 1), i, :], we).then_inc(we_in, 16)

            def load_items(j, jj):
                wait(sp, alpha_done, GB * (j - 1))
                sp.dma_start(erec[:, jj, :], erec_dram[bass.ds(j, 1), :, :].rearrange("a e f -> (a e) f")).then_inc(erec_in[jj], 16)

            def load_pens(j, jj):
                wait(sp, max_done, j - 1)
                wait(sp, run_b, j - 1)
                for h in range(H):
                    sp.dma_start(pen[BI * h:BI * (h + 1), jj, :], pen_dram[bass.ds(j * BI, BI), :]).then_inc(pen_in[jj], 16)
                sp.dma_start(cpr[0:1, jj, :, :].rearrange("a d f -> a (d f)"),
                             cp_dram[bass.ds(j, 1), :, :].rearrange("a d f -> a (d f)")).then_inc(pen_in[jj], 16)

            def step(turn, s, table, tile0):
                n = UNR * turn + s
                jj = s // GB
                j = 2 * turn + jj
                wait(sp, at_ps, n - SLOTS + 1)
                blocks = blocks_of(EngineType.SP, n)
                for i in range(GI):
                    tile = nc.s_assert_within(GI * n + i - blocks[i] - tile0, 0, table.shape[0] // P - 1, skip_runtime_bounds_check_because=(
                        "item i's tile is i - b[i], from 0 to the tile that item i would have with b = 0"))
                    sp.dma_start(araw[:, s % SLOTS, i, :], table[bass.ds(tile * P, P), :]).then_inc(attr_in[s % SLOTS], 16)
                if s % GB == 3:
                    load_pens(j, jj)
                if s % GB == 5 and not (isinstance(j, int) and j + 1 >= NBATCH):
                    load_items(j + 1, 1 - jj)

            load_items(0, 0)
            for s in range(UNR):
                step(0, s, attr, 0)
            whole = (NBATCH - 4) // 2
            with sp.Fori(1, whole) as turn:
                for s in range(UNR):
                    step(turn, s, attr, 0)
            for turn in range(whole, TURNS):
                for s in range(UNR):
                    step(turn, s, tail_dram, TAIL0)

        @block.gpsimd
        def _(pool):
            nc.gpsimd.memset(we4[:], 0.0).then_inc(setup, 1)
            nc.gpsimd.iota(iota_i, pattern=[[1, P]], base=0, channel_multiplier=0).then_inc(setup, 1)
            nc.gpsimd.memset(sel4[:], 0.0).then_inc(setup, 1)
            nc.gpsimd.memset(one[:], 1.0).then_inc(setup, 1)
            nc.gpsimd.memset(zb[:], -BIG).then_inc(setup, 1)
            nc.gpsimd.memset(rf[:], -BIG).then_inc(setup, 1)
            pool.wait_ge(setup, 6)
            nc.gpsimd.tensor_copy(iota_f[:], iota_i).then_inc(setup, 1)
            nc.gpsimd.affine_select(out=sel4[:], in_=sel4[:], compare_op=ALU.not_equal, fill=1.0, base=0,
                                    pattern=[[-BI, H]], channel_multiplier=1).then_inc(setup, 1)
            nc.gpsimd.memset(val[:, :, :, :, C:CW], 1.0).then_inc(setup, 1)
            nc.gpsimd.memset(acc[:], 0.0).then_inc(setup, 1)

            def step(turn, s):
                n = UNR * turn + s
                jj = s // GB
                batch = ((erec_in[jj], 16 * (turn + 1)),) if s % GB == 0 else ()
                wait_apart(pool, setup, (alpha_done, n - SLOTS + 1), *batch)
                for i in range(GI):
                    t = GI * (s % GB) + i
                    nc.gpsimd.indirect_dma_start(
                        out=kvr[:, s % SLOTS, i, :], out_offset=None, in_=kv_dram,
                        in_offset=bass.IndirectOffsetOnAxis(ap=erec[:, jj, t:t + 1], axis=0)).then_inc(kv_in[s % SLOTS], 16)

            for s in range(UNR):
                step(0, s)
            with pool.Fori(1, TURNS) as turn:
                for s in range(UNR):
                    step(turn, s)

        @block.vector
        def _(dve):
            V = nc.vector

            def add_item(turn, s, i, blocks):
                n = UNR * turn + s - LAG - 1
                if not live(n) or i not in range(GI):
                    return
                rows = acc[:, bass.ds(blocks[i], 1), :]
                if i % 2 == 0:
                    dve.wait_ge(agg_ps, 2 * n + i // 2 + 1)
                if i == 0 and starts_batch(s):
                    dve.wait_ge(scaled, 2 * turn + (s - LAG - 1) // GB + 1)
                wait(dve, acc_done, GI * n + i)
                rows = rows.rearrange("p a f -> p (a f)")
                V.tensor_tensor(rows, rows, p_ag[i // 2][:, (i % 2) * 256:(i % 2) * 256 + H * CW], ALU.add).then_inc(acc_done, 1)

            def rescale(turn, s, blocks):
                n = UNR * turn + s - LAG - 1
                if not live(n):
                    return
                wait(dve, acc_done, GI * n)
                dve.wait_ge(f_done, 2 * turn + (s - LAG - 1) // GB + 1)
                rows = acc[:, bass.ds(blocks[0], 1), :].rearrange("p a (h c) -> p (a h) c", c=CW)
                V.tensor_tensor(rows, rows, fac[:].unsqueeze(2).broadcast_to([P, H, CW]), ALU.mult).then_inc(scaled, 1)

            def starts_batch(s):
                return (s - LAG - 1) % GB == 0

            def softmax(turn, s, place):
                j, jj = behind(turn, s)
                if j is None:
                    return
                at_ = (s % GB, place)
                al = p_al[:, 0:P]
                if at_ == (0, 0):
                    dve.wait_ge(al_ps, j + 1)
                    wait(dve, ex_ps, j)
                    dve.wait_ge(pen_in[jj], 16 * PENS * (turn + s // GB))
                    V.tensor_tensor_scan(fwd[:], pen[:, jj, 0:P], al, -BIG, ALU.add, ALU.max).then_inc(last_f, 1)
                    V.tensor_copy(zf[:, :, 0], rf[:, :, BI]).then_inc(carry_f, 1)
                elif at_ == (0, 1):
                    dve.wait_ge(row_f, j + 1)
                    V.tensor_copy(zf[:, :, 1:CW], p_row.rearrange("a (h t) -> a h t", h=H)).then_inc(z_f, 1)
                elif at_ == (0, 2):
                    dve.wait_ge(carry_f, j + 1)
                    dve.wait_ge(z_f, j + 1)
                    V.tensor_tensor_scan(rf[:].rearrange("a h t -> a (h t)"), cpr[0:1, jj, 0, :],
                                         zf[:].rearrange("a h t -> a (h t)"), -BIG, ALU.add, ALU.max).then_inc(run_f, 1)
                elif at_ == (1, 0):
                    dve.wait_ge(col_f, j + 1)
                    V.tensor_copy(cin[:, 0:1], p_col).then_inc(cin_f, 1)
                elif at_ == (1, 1):
                    dve.wait_ge(cin_f, j + 1)
                    V.tensor_tensor_scan(fwd[:], pen[:, jj, 0:P], al, cin[:, 0:1], ALU.add, ALU.max).then_inc(fwd_done, 1)
                elif at_ == (1, 2):
                    dve.wait_ge(fwd_done, j + 1)
                    V.tensor_tensor_scan(bwd[:, ::-1], pen[:, jj, P:0:-1], fwd[:, ::-1], -BIG, ALU.add, ALU.max).then_inc(first_b, 1)
                elif at_ == (2, 0):
                    dve.wait_ge(row_b, j + 1)
                    V.tensor_copy(zb[:, :, 0:BI], p_row.rearrange("a (h t) -> a h t", h=H)).then_inc(z_b, 1)
                elif at_ == (2, 1):
                    dve.wait_ge(z_b, j + 1)
                    V.tensor_tensor_scan(zb[:].rearrange("a h t -> a (h t)")[:, ::-1], cpr[0:1, jj, 1, ::-1],
                                         zb[:].rearrange("a h t -> a (h t)")[:, ::-1], -BIG, ALU.add, ALU.max).then_inc(run_b, 1)
                elif at_ == (3, 0):
                    dve.wait_ge(col_b, j + 1)
                    V.tensor_copy(cin[:, 1:2], p_col).then_inc(cin_b, 1)
                elif at_ == (3, 1):
                    dve.wait_ge(cin_b, j + 1)
                    V.tensor_tensor_scan(bwd[:, ::-1], pen[:, jj, P:0:-1], fwd[:, ::-1], cin[:, 1:2], ALU.add, ALU.max).then_inc(max_done, 1)
                elif at_ == (3, 2):
                    dve.wait_ge(max_done, j + 1)
                    V.tensor_tensor(fwd[:], al, bwd[:], ALU.subtract).then_inc(diff_done, 1)
                elif at_ == (4, 0):
                    dve.wait_ge(m_ps, j + 1)
                    V.tensor_tensor(dm[:, 0, :], zf[:, :, 0], p_m, ALU.subtract).then_inc(dm_sub, 1)
                elif at_ == (4, 1):
                    dve.wait_ge(dm_sub, j + 1)
                    V.tensor_scalar(dm[:, 1, :], dm[:, 0, :], 0.0, None, ALU.min).then_inc(dm_done, 1)

            def step(turn, s):
                n = UNR * turn + s
                jj = s // GB
                j = 2 * turn + jj
                slot = s % SLOTS
                here = live(n)
                kpart = kvr[:, slot, :, 0:D]
                blocks = blocks_of(EngineType.DVE, n - LAG - 1) if live(n - LAG - 1) else None
                if here:
                    dve.wait_ge(kv_in[slot], 16 * GI * (UNR // SLOTS * turn + s // SLOTS + 1))
                    dve.wait_ge(e_ps, n + 1)
                    pe_ = p_e[:].rearrange("e (i c) -> e i c", i=GI)
                    V.tensor_tensor(kpart, kpart, pe_, ALU.add).then_inc(k_done, 1)
                late = 1 if starts_batch(s) else 0
                add_item(turn, s, 0 - late, blocks)
                if here:
                    V.tensor_tensor(val[:, s % RING, :, :, 0:C], kvr[:, slot, :, D:2 * D].rearrange("e i (h c) -> e i h c", h=H),
                                    p_e[:].rearrange("e (i h c) -> e i h c", i=GI, h=H), ALU.add).then_inc(v_done, 1)
                if late:
                    rescale(turn, s, blocks)
                add_item(turn, s, 1 - 2 * late, blocks)
                softmax(turn, s, 0)
                if here:
                    dve.wait_ge(q_ps, n + 1)
                    dve.wait_ge(k_done, n + 1)
                    V.tensor_tensor(kpart, kpart, p_qd[:].rearrange("e (i c) -> e i c", i=GI), ALU.mult).then_inc(prod_done, 1)
                add_item(turn, s, 2 - 2 * late, blocks)
                m = n - LAG
                if live(m):
                    sm = (s - LAG) % RING
                    jb = 2 * turn + (s - LAG) // GB
                    t0 = GI * ((s - LAG) % GB)
                    dve.wait_ge(ex_done, jb + 1)
                    wait(dve, agg_ps, 2 * (m - 1))
                    dve.wait_ge(v_done, m + 1)
                    V.tensor_tensor(wv[:, s % 2, :, :].rearrange("e i (h c) -> e i h c", h=H), val[:, sm, :, :, :],
                                    ex[:, ((s - LAG) // GB) % 2, :, t0:t0 + GI].rearrange("e h i -> e i h").unsqueeze(3)
                                    .broadcast_to([P, GI, H, CW]), ALU.mult).then_inc(wv_done, 1)
                if late:
                    add_item(turn, s, 1, blocks)
                softmax(turn, s, 1)
                add_item(turn, s, 3 - late, blocks)
                if here:
                    dve.wait_ge(prod_done, n + 1)
                    if s % GB == 0:
                        wait(dve, al_ps, j - 1)
                    t0 = GI * (s % GB)
                    V.tensor_reduce(alpha[:, jj, :, t0:t0 + GI].rearrange("e h i -> e i h"),
                                    kpart.rearrange("e i (h c) -> e i h c", h=H), axis=AX.X, op=ALU.add).then_inc(alpha_done, 1)
                if late:
                    add_item(turn, s, 3, blocks)
                softmax(turn, s, 2)

            dve.wait_ge(setup, 10)
            for s in range(UNR):
                step(0, s)
            with dve.Fori(1, TURNS) as turn:
                for s in range(UNR):
                    step(turn, s)
            for s in range(STEPS_LEFT):
                step(TURNS, s)

        @block.scalar
        def _(act):
            S = nc.scalar

            def one_hots(turn, s):
                n = UNR * turn + s
                if not live(n):
                    return
                jj = (s // GB) % 2
                slot = s % RING
                act.wait_ge(erec_in[jj], 16 * (turn + s // UNR + 1))
                wait(act, agg_ps, 2 * (n - RING + 1))
                for i in range(GI):
                    t = BI + GI * (s % GB) + i
                    last = S.activation(onehot[:, slot, i, :], iota_f[:], ACT.Square, bias=erec[:, jj, t:t + 1].bitcast(F32))
                last.then_inc(sq_done, 1)
                act.wait_ge(sq_done, n + 1)
                S.activation(onehot[:, slot, :, :], onehot[:, slot, :, :], ACT.Relu, scale=-1.0, bias=1.0).then_inc(onehot_done, 1)

            def copies(turn, s):
                n = UNR * turn + s
                if not live(n):
                    return
                act.wait_ge(at_ps, n + 1)
                wait(act, e_ps, n)
                S.activation(at[:], p_at[:, 0:P], ACT.Copy).then_inc(at_sb, 1)
                act.wait_ge(st_ps, n + 1)
                wait(act, q_ps, n)
                S.activation(st[:].rearrange("p i e -> p (i e)"), p_st[:], ACT.Copy).then_inc(st_sb, 1)

            def step(turn, s):
                j, jj = behind(turn, s)
                if s % GB == 4 and j is not None:
                    act.wait_ge(diff_done, j + 1)
                    S.activation(fwd[:], fwd[:], ACT.Exp, scale=SCALE).then_inc(ext_done, 1)
                    act.wait_ge(ex_ps, j + 1)
                    wait(act, wv_done, GB * (j - 1))
                    S.activation(ex[:, jj, :, :].rearrange("e h t -> e (h t)"), p_ex, ACT.Copy).then_inc(ex_done, 1)
                copies(turn, s + 1)
                one_hots(turn, s + 2)
                if s % GB == 4 and j is not None:
                    act.wait_ge(f_ps, j + 1)
                    wait(act, scaled, j)
                    S.activation(fac[:], p_f, ACT.Exp, scale=SCALE).then_inc(f_done, 1)

            act.wait_ge(setup, 7)
            one_hots(0, 0)
            copies(0, 0)
            one_hots(0, 1)
            for s in range(UNR):
                step(0, s)
            with act.Fori(1, TURNS - 1) as turn:
                for s in range(UNR):
                    step(turn, s)
            for s in range(UNR):
                step(TURNS - 1, s)
            for s in range(STEPS_LEFT):
                step(TURNS, s)

        @block.tensor
        def _(pe):
            T = nc.tensor

            def transposes(turn, s):
                n = UNR * turn + s
                if not live(n):
                    return
                slot = s % SLOTS
                pe.wait_ge(attr_in[slot], 16 * GI * (UNR // SLOTS * turn + s // SLOTS + 1))
                wait(pe, at_sb, n)
                T.transpose(p_at[:, 0:P], araw[:, slot, :, :].rearrange("e i a -> e (i a)"), ident[:]).then_inc(at_ps, 1)
                pe.wait_ge(onehot_done, n + 1)
                wait(pe, st_sb, n)
                for i in range(GI):
                    last = T.transpose(p_st[:, i * P:(i + 1) * P], onehot[:, s % RING, i, :], ident[:])
                last.then_inc(st_ps, 1)

            def edge_terms(turn, s):
                n = UNR * turn + s
                if not live(n):
                    return
                pe.wait_ge(at_sb, n + 1)
                wait(pe, v_done, n)
                T.matmul(p_e[:], at[:], we4[:].rearrange("a i c -> a (i c)"), start=True, stop=True).then_inc(e_ps, 1)

            def queries(turn, s):
                n = UNR * turn + s
                if not live(n):
                    return
                blocks = blocks_of(EngineType.PE, n)
                pe.wait_ge(st_sb, n + 1)
                wait(pe, prod_done, n)
                for i in range(GI):
                    last = T.matmul(p_qd[:, i * P:(i + 1) * P], st[:, i, :], qt[:, bass.ds(blocks[i], 1), :].rearrange("p a d -> p (a d)"),
                                    start=True, stop=True)
                last.then_inc(q_ps, 1)

            def sums(turn, s):
                n = UNR * turn + s
                if not live(n):
                    return
                pe.wait_ge(wv_done, n + 1)
                for i in range(GI):
                    if i % 2 == 0:
                        wait(pe, acc_done, GI * (n - 1) + i + 2)
                    last = T.matmul(p_ag[i // 2][:, (i % 2) * 256:(i % 2) * 256 + H * CW], onehot[:, s % RING, i, :],
                                    wv[:, s % 2, i, :], start=True, stop=True)
                    if i % 2 == 1:
                        last.then_inc(agg_ps, 1)

            def softmax(turn, s, place):
                j, jj = behind(turn, s)
                if j is None:
                    return
                at_ = (s % GB, place)
                if at_ == (0, 0):
                    pe.wait_ge(alpha_done, GB * (j + 1))
                    wait(pe, ex_done, j)
                    T.transpose(p_al[:, 0:P], alpha[:, jj, :, :].rearrange("e h t -> e (h t)"), ident[:]).then_inc(al_ps, 1)
                elif at_ == (0, 1):
                    pe.wait_ge(last_f, j + 1)
                    wait(pe, f_done, j)
                    T.matmul(p_row, fwd[:, P - 1:P], ident[:], start=True, stop=True).then_inc(row_f, 1)
                elif at_ == (1, 0):
                    wait_apart(pe, setup, (run_f, j + 1))
                    for h in range(H):
                        last = T.matmul(p_col[BI * h:BI * (h + 1), :], rf[0:1, h, 0:BI], one[:], start=True, stop=True)
                    last.then_inc(col_f, 1)
                elif at_ == (2, 0):
                    pe.wait_ge(first_b, j + 1)
                    T.matmul(p_row, bwd[:, 0:1], ident[:], start=True, stop=True).then_inc(row_b, 1)
                elif at_ == (3, 0):
                    wait_apart(pe, setup, (run_b, j + 1))
                    for h in range(H):
                        last = T.matmul(p_col[BI * h:BI * (h + 1), :], zb[0:1, h, 1:CW], one[:], start=True, stop=True)
                    last.then_inc(col_b, 1)
                elif at_ == (4, 0):
                    pe.wait_ge(max_done, j + 1)
                    T.matmul(p_m, bwd[:, 0:1], sel4[:], start=True, stop=True).then_inc(m_ps, 1)
                    pe.wait_ge(ext_done, j + 1)
                    T.transpose(p_ex, fwd[:], ident[:]).then_inc(ex_ps, 1)
                elif at_ == (4, 2):
                    pe.wait_ge(dm_done, j + 1)
                    T.matmul(p_f, onehot[0:1, jj * GB, 0, :], dm[:, 1, :], start=True, stop=True).then_inc(f_ps, 1)

            def step(turn, s):
                softmax(turn, s, 0)
                transposes(turn, s + 1)
                edge_terms(turn, s + 1)
                softmax(turn, s, 1)
                queries(turn, s + 1)
                sums(turn, s - LAG)
                softmax(turn, s, 2)

            pe.wait_ge(setup, 8)
            pe.wait_ge(we_in, 16 * GI)
            transposes(0, 0)
            edge_terms(0, 0)
            queries(0, 0)
            for s in range(UNR):
                step(0, s)
            with pe.Fori(1, TURNS - 1) as turn:
                for s in range(UNR):
                    step(turn, s)
            for s in range(UNR):
                step(TURNS - 1, s)
            for s in range(STEPS_LEFT):
                step(TURNS, s)


def output(nc, x, w1, b1, w2, b2, out, dram, acc, ident):
    skip_dram = dram[1]
    WID = 4
    WHOLE = NB // WID
    REST = NB - WHOLE * WID
    BUFS = 4
    TURNS = WHOLE // BUFS

    with ExitStack() as ctx:
        def sb(name, shape, dt=F32):
            return ctx.enter_context(nc.sbuf_tensor(name, shape, dt))

        def sem(name):
            return ctx.enter_context(nc.semaphore(name))

        xs = sb("x3", [P, BUFS, WID, D])
        sk = sb("skip3", [P, BUFS, WID, D])
        w1s, w2s = sb("w1s", [P, D]), sb("w2s", [P, D])
        b1s, b2s = sb("b1s", [P, 1]), sb("b2s", [P, 1])
        den = sb("den", [P, NB, H])
        o = sb("o", [P, BUFS, WID, D])
        ot = sb("ot", [P, WID * P])
        h1 = sb("h1", [P, WID * P])
        h2 = sb("h2", [P, WID * P])
        res = sb("res", [P, BUFS, WID, D])
        p_o, p_1, p_2, p_3 = (ctx.enter_context(nc.psum_tensor(f"p3_{i}", [P, 512], F32)) for i in range(4))
        x_loaded = [sem(f"x_loaded{i}") for i in range(BUFS)]
        skip_loaded = [sem(f"skip_loaded{i}") for i in range(BUFS)]
        w_in3 = sem("w_in3")
        den_add, den_inv, normed, out_ready, xo_ready = (sem(n) for n in ("den_add", "den_inv", "normed", "out_ready", "xo_ready"))
        ot_ps, ot_sb, h1_ps, h1_sb, h2_ps, h2_sb, y_ps, res_ready = (
            sem(n) for n in ("ot_ps", "ot_sb", "h1_ps", "h1_sb", "h2_ps", "h2_sb", "y_ps", "res_ready"))
        out_stored = [sem(f"out_stored{i}") for i in range(BUFS)]
        block = ctx.enter_context(nc.Block())

        def whole(g):
            return not isinstance(g, int) or 0 <= g < WHOLE

        def width(g):
            return WID if whole(g) else REST if g == WHOLE else 0

        def each_step(engine, step, left):
            for s in range(BUFS):
                step(0, s)
            with engine.Fori(1, TURNS - 1) as turn:
                for s in range(BUFS):
                    step(turn, s)
            for turn in range(TURNS - 1, TURNS + 1):
                for s in range(BUFS if turn < TURNS else left):
                    step(turn, s)

        r0, r1 = WHOLE * WID * P, (NB - 1) * P

        def load(sp, g, k, buffer, table, loaded):
            if whole(g):
                rows = bass.ds(g * (WID * P), WID * P)
                sp.dma_start(buffer[:, k, :, :], table[rows, :].rearrange("(u p) d -> p u d", p=P)).then_inc(loaded, 16)
            elif width(g):
                sp.dma_start(buffer[:, k, 0:REST - 1, :], table[r0:r1, :].rearrange("(u p) d -> p u d", p=P)).then_inc(loaded, 16)
                sp.dma_start(buffer[0:N - r1, k, REST - 1, :], table[r1:N, :]).then_inc(loaded, 16)

        @block.sync
        def _(sp):
            for k in range(BUFS):
                load(sp, k, k, sk, skip_dram, skip_loaded[k])
                load(sp, k, k, xs, x, x_loaded[k])
                if k == 0:
                    sp.dma_start(w1s[:], w1).then_inc(w_in3, 16)
                    sp.dma_start(w2s[:], w2).then_inc(w_in3, 16)
                    sp.dma_start(b1s[:], b1.rearrange("(c a) -> c a", a=1)).then_inc(w_in3, 16)
                    sp.dma_start(b2s[:], b2.rearrange("(c a) -> c a", a=1)).then_inc(w_in3, 16)

            def step(turn, s):
                g = BUFS * turn + s
                if width(g + BUFS):
                    sp.wait_ge(out_ready, g + 1)
                    load(sp, g + BUFS, s, sk, skip_dram, skip_loaded[s])
                    sp.wait_ge(xo_ready, g + 1)
                    load(sp, g + BUFS, s, xs, x, x_loaded[s])
                sp.wait_ge(res_ready, g + 1)
                if whole(g):
                    sp.dma_start(out[bass.ds(g * (WID * P), WID * P), :].rearrange("(u p) d -> p u d", p=P), res[:, s, :, :]
                                 ).then_inc(out_stored[s], 16)
                else:
                    sp.dma_start(out[r0:r1, :].rearrange("(u p) d -> p u d", p=P), res[:, s, 0:REST - 1, :]).then_inc(out_stored[s], 16)
                    sp.dma_start(out[r1:N, :], res[0:N - r1, s, REST - 1, :]).then_inc(out_stored[s], 16)

            each_step(sp, step, 1)
            for k in range(BUFS):
                sp.wait_ge(out_stored[k], 16 * TURNS + (32 if k == WHOLE % BUFS else 0))

        @block.gpsimd
        def _(pool):
            def step(turn, s):
                g = BUFS * turn + s
                w = width(g)
                pool.wait_ge(out_ready, g + 1)
                pool.wait_ge(x_loaded[s], 16 * (turn + 1) + 16 * (w < WID))
                wait(pool, out_stored[s], 16 * turn)
                nc.gpsimd.tensor_tensor(res[:, s, 0:w, :], o[:, s, 0:w, :], xs[:, s, 0:w, :], ALU.add).then_inc(xo_ready, 1)

            each_step(pool, step, 1)

        @block.vector
        def _(dve):
            V = nc.vector
            sums = acc[:].rearrange("p b (h c) -> p b h c", c=CW)
            V.tensor_scalar(den[:], sums[:, :, :, C], EPS_SUM, None, ALU.add).then_inc(den_add, 1)
            dve.wait_ge(den_add, 1)
            V.reciprocal(den[:], den[:]).then_inc(den_inv, 1)
            dve.wait_ge(den_inv, 1)

            def step(turn, s):
                g = BUFS * turn + s
                w = width(g)
                if w:
                    rows = acc[:, bass.ds(g * WID, w), :].rearrange("p u (h c) -> p u h c", c=CW)
                    wait(dve, ot_ps, g - BUFS + 1)
                    wait(dve, xo_ready, g - BUFS + 1)
                    V.tensor_tensor(o[:, s, 0:w, :].rearrange("p u (h c) -> p u h c", h=H), rows[:, :, :, 0:C],
                                    den[:, bass.ds(g * WID, w), :].unsqueeze(3).broadcast_to([P, w, H, C]), ALU.mult).then_inc(normed, 1)
                v, k = width(g - 3), (s - 3) % BUFS
                if v:
                    dve.wait_ge(y_ps, g - 2)
                    dve.wait_ge(xo_ready, g - 2)
                    V.tensor_tensor(res[:, k, 0:v, :].rearrange("p u d -> p (u d)"), res[:, k, 0:v, :].rearrange("p u d -> p (u d)"),
                                    p_3[:, 0:v * D], ALU.add).then_inc(res_ready, 1)
                if w:
                    dve.wait_ge(normed, g + 1)
                    dve.wait_ge(skip_loaded[s], 16 * (turn + 1) + 16 * (w < WID))
                    V.tensor_tensor(o[:, s, 0:w, :], o[:, s, 0:w, :], sk[:, s, 0:w, :], ALU.add).then_inc(out_ready, 1)

            each_step(dve, step, 4)

        @block.scalar
        def _(act):
            S = nc.scalar

            def transposed(g):
                m = width(g) * P
                if m:
                    act.wait_ge(ot_ps, g + 1)
                    wait(act, h1_ps, g)
                    S.activation(ot[:, 0:m], p_o[:, 0:m], ACT.Copy).then_inc(ot_sb, 1)

            def step(turn, s):
                g = BUFS * turn + s
                m = width(g) * P
                act.wait_ge(h1_ps, g + 1)
                S.activation(h1[:, 0:m], p_1[:, 0:m], ACT.Gelu_apprx_tanh, bias=b1s[:, 0:1]).then_inc(h1_sb, 1)
                transposed(g + 1)
                act.wait_ge(h2_ps, g + 1)
                wait(act, y_ps, g)
                S.activation(h2[:, 0:m], p_2[:, 0:m], ACT.Gelu_apprx_tanh, bias=b2s[:, 0:1]).then_inc(h2_sb, 1)

            act.wait_ge(w_in3, 64)
            transposed(0)
            each_step(act, step, 1)

        @block.tensor
        def _(pe):
            T = nc.tensor

            def transposes_in(g, k):
                if width(g):
                    pe.wait_ge(out_ready, g + 1)
                    wait(pe, ot_sb, g)
                    for u in range(width(g)):
                        last = T.transpose(p_o[:, u * P:(u + 1) * P], o[:, k, u, :], ident[:])
                    last.then_inc(ot_ps, 1)

            def transposes_out(g):
                if width(g):
                    pe.wait_ge(h2_sb, g + 1)
                    wait(pe, res_ready, g)
                    for u in range(width(g)):
                        last = T.transpose(p_3[:, u * P:(u + 1) * P], h2[:, u * P:(u + 1) * P], ident[:])
                    last.then_inc(y_ps, 1)

            def step(turn, s):
                g = BUFS * turn + s
                m = width(g) * P
                if m:
                    pe.wait_ge(ot_sb, g + 1)
                    wait(pe, h1_sb, g)
                    T.matmul(p_1[:, 0:m], w1s[:], ot[:, 0:m], start=True, stop=True).then_inc(h1_ps, 1)
                transposes_out(g - 1)
                transposes_in(g + 1, (s + 1) % BUFS)
                if m:
                    pe.wait_ge(h1_sb, g + 1)
                    wait(pe, h2_sb, g)
                    T.matmul(p_2[:, 0:m], w2s[:], h1[:, 0:m], start=True, stop=True).then_inc(h2_ps, 1)

            pe.wait_ge(w_in3, 64)
            transposes_in(0, 0)
            each_step(pe, step, 2)


def graph_transformer(nc, x, src, dst, attr, wq, bq, wk, bk, wv, bv, we, wskip, bskip, w1, b1, w2, b2, out):
    def scratch(name, shape, dt=F32):
        return nc.dram_tensor(name, shape, dt, kind="Internal").ap()

    dram = (scratch("kv_rows", (N, 2 * D)), scratch("skip_rows", (N, D)),
            scratch("dst_tiles", (NI, P), I32), scratch("src_tiles", (NI, P), I32),
            scratch("tags", (NI * P + 2,)), scratch("penalties", (NI, P + 1)),
            scratch("carry_penalties", (NBATCH, 2, H * CW)), scratch("item_edges", (NBATCH, P, 2 * BI), I32),
            scratch("item_blocks", (NI,), I32), scratch("attr_end", (NTAIL * P, A)))
    with ExitStack() as ctx:
        acc = ctx.enter_context(nc.sbuf_tensor("acc", [P, NB, H * CW], F32))
        ident = ctx.enter_context(nc.sbuf_tensor("ident", [P, P], F32))
        with ExitStack() as inner:
            qt = inner.enter_context(nc.sbuf_tensor("qt", [P, NB, D], F32))
            brow = inner.enter_context(nc.sbuf_tensor("brow", [1, NI], I32))
            index_and_nodes(nc, x, src, dst, attr, wq, bq, wk, bk, wv, bv, wskip, bskip, dram, qt, acc, ident, brow)
            edges(nc, attr, we, dram, qt, acc, ident, brow)
        output(nc, x, w1, b1, w2, b2, out, dram, acc, ident)


_INS = ['x', 'src', 'dst', 'edge_attr_32', 'L0_gnn_Wq', 'L0_gnn_bq', 'L0_gnn_Wk', 'L0_gnn_bk', 'L0_gnn_Wv', 'L0_gnn_bv',
        'L0_gnn_We', 'L0_gnn_Wskip', 'L0_gnn_bskip', 'L0_gnn_W1', 'L0_gnn_b1', 'L0_gnn_W2', 'L0_gnn_b2']
_OUTS = [((12500, 128), 'float32')]


def kernel(**inputs):
    import numpy as _np
    import concourse.bacc as _bacc
    from concourse import mybir as _mybir
    from concourse.bass_utils import run_bass_kernel_spmd as _run

    nc = _bacc.Bacc("TRN2", target_bir_lowering=False, num_devices=1)
    arrays, args = {}, []
    for name in _INS:
        a = _np.ascontiguousarray(inputs[name])
        arrays[f"in_{name}_dram"] = a
        args.append(nc.dram_tensor(f"in_{name}_dram", a.shape, _mybir.dt.from_np(a.dtype), kind="ExternalInput").ap())
    for i, (shape, dtype) in enumerate(_OUTS):
        dt = _mybir.dt.from_np(_np.dtype(dtype))
        args.append(nc.dram_tensor(f"out_{i}_dram", shape, dt, kind="ExternalOutput").ap())
    graph_transformer(nc, *args)
    r = _run(nc, [arrays], core_ids=[0])
    got = tuple(r.results[0][f"out_{i}_dram"] for i in range(len(_OUTS)))
    return got[0]
```

```python
from contextlib import ExitStack

import concourse.bass as bass
from concourse import mybir

F32 = mybir.dt.float32
I32 = mybir.dt.int32
ALU = mybir.AluOpType
ACT = mybir.ActivationFunctionType
AX = mybir.AxisListType
EngineType = mybir.EngineType

P = 128
N, E, D, H, A = 12500, 200000, 128, 4, 32
C = D // H
CW = C + 1
NB = -(-N // P)
NT = -(-E // P)
GI = 4
BI = 32
GB = BI // GI
NBATCH = -(-(NT + NB - 1) // BI)
NI = NBATCH * BI
NC = NI // P
NG = NI // GI
SLOTS = 4
RING = 2 * GB
LAG = GB + GB // 2
PAD = 1 << 14
BIG = 1.0e30
SCALE = float(C) ** -0.5
EPS_LN, EPS_SUM = 1e-5, 1e-16
TAIL0 = (NBATCH - 4) * BI - NB
NTAIL = NI - (NBATCH - 4) * BI + NB
CB = 7
NCH = NB // CB


def wait(engine, semaphore, value):
    if not isinstance(value, int) or value > 0:
        engine.wait_ge(semaphore, value)


def wait_apart(engine, reached, *waits):
    for semaphore, value in waits:
        if not isinstance(value, int):
            engine.to_reg(value)
    engine.wait_ge(reached, 1)
    for semaphore, value in waits:
        wait(engine, semaphore, value)


def live(group):
    return not isinstance(group, int) or 0 <= group < NG


def index_and_nodes(nc, x, src, dst, attr, wq, bq, wk, bk, wv, bv, wskip, bskip, dram, qt, acc, ident, brow):
    kv_dram, skip_dram, dst_dram, src_dram, tag_dram, pen_dram, cp_dram, erec_dram, brow_dram, tail_dram = dram
    NQ = 4 * D
    FULL = (NT // P) * P
    REST = E // P - FULL
    LAST = E - (FULL + REST) * P

    with ExitStack() as ctx:
        def sb(name, shape, dt=F32):
            return ctx.enter_context(nc.sbuf_tensor(name, shape, dt))

        def sem(name):
            return ctx.enter_context(nc.semaphore(name))

        flat, used = acc[:].rearrange("p b f -> p (b f)"), [0]

        def part(shape):
            at, size = used[0], shape[0] * shape[1]
            used[0] += size
            return flat[:, at:at + size].rearrange("p (a b) -> p a b", a=shape[0])

        xs = sb("xs", [P, 2, CB, D])
        w4 = sb("w4", [P, NQ])
        bias4 = sb("bias4", [P, NQ])
        stats = sb("stats", [P, 2, CB, 6])
        mv = sb("mv", [P, 2, CB, 2])
        std = sb("std", [P, 2, CB])
        rstd = sb("rstd", [P, 2, CB])
        shift = sb("shift", [P, 2, CB])
        eps = sb("eps", [P, 1])
        xn = sb("xn", [P, 2, D])
        ht = sb("ht", [P, 2, P])
        nodes = sb("nodes", [P, 2, CB, 3 * D])

        dt_i = sb("dt_i", [P, NC, P], I32)
        st_i = sb("st_i", [P, NC, P], I32)
        di_i = sb("di_i", [P, NC, P], I32)
        si_i = sb("si_i", [P, NC, P], I32)
        di = part([NC, P])
        si = part([NC, P])
        ndl = sb("ndl", [P, NC, P])
        tag = part([NC, P])
        tagp = part([NC, P])
        tagn = part([NC, P])
        lastd = sb("lastd", [P, NC])
        kint = sb("kint", [P, NB], I32)
        kf = sb("kf", [P, NB])
        k128 = sb("k128", [P, NB])
        iint = sb("iint", [P, NC], I32)
        ifl = sb("ifl", [P, NC])
        cmp1 = part([NB, NC])
        cmp2 = part([NC, NB])
        cnt = sb("cnt", [P, NB])
        start = sb("start", [P, NB])
        ones = sb("ones", [P, P])
        bsum = sb("bsum", [P, NC])
        bf = sb("bf", [P, NC])
        b128 = sb("b128", [P, NC])
        btag = sb("btag", [P, NC])
        tf = sb("tf", [P, NC])
        ti = sb("ti", [P, NC], I32)
        cp = sb("cp", [P, 2, NC])
        cpx = sb("cpx", [NC, 2, 4, H, CW])
        bti = sb("bti", [NC, P], I32)
        cap = sb("cap", [1, 1])
        erec = sb("erec", [P, NC, 4, 2 * BI], I32)

        PARTS = ((0, 2), (2, 4), (4, CB))
        AHEAD = CB + 4

        with ExitStack() as pctx:
            def pb(name, shape):
                return pctx.enter_context(nc.psum_tensor(name, shape, F32))

            p_t = [pb(f"p_t{i}", [P, 512]) for i in range(2)]
            p_q = [pb(f"p_q{i}", [P, NQ]) for i in range(2)]
            p_i = pb("p_i", [P, 512])
            p_tr = [pb(f"p_tr{i}", [P, 512]) for i in range(2)]

            x_in = [[sem(f"x_in{i}_{part}") for part in range(len(PARTS))] for i in range(2)]
            w_in = sem("w_in")
            stored = [sem(f"stored{i}") for i in range(2)]
            d_in, s_in = sem("d_in"), sem("s_in")
            scratch_out = sem("scratch_out")
            di_in, si_in = sem("di_in"), sem("si_in")
            tag_out, tagp_in, pen_out, idx_out, brow_out, brow_in = (
                sem(n) for n in ("tag_out", "tagp_in", "pen_out", "idx_out", "brow_out", "brow_in"))
            pads, consts, iotas, caps = sem("pads"), sem("consts"), sem("iotas"), sem("caps")
            chain, table_chain, tag_diff = sem("index_chain"), sem("table_chain"), sem("tag_diff")
            cnt_ready, count_ps, ti_ready, pen_ready, cp_ready = (
                sem(n) for n in ("cnt_ready", "count_ps", "ti_ready", "pen_ready", "cp_ready"))
            tables_f, tr_ps, tr_sb, small_ps, small_sb = (sem(n) for n in ("tables_f", "tr_ps", "tr_sb", "small_ps", "small_sb"))
            stats_done, aggr_done, std_done, rstd_done, shift_done = (
                sem(n) for n in ("stats_done", "aggr_done", "std_done", "rstd_done", "shift_done"))
            xn_ready, xt_ps, ht_ready, qkvs_ps, qkvs_out = (sem(n) for n in ("xn_ready", "xt_ps", "ht_ready", "qkvs_ps", "qkvs_out"))
            block = pctx.enter_context(nc.Block())

            PAIRS = NCH // 2
            MID = 4
            TR = -(-NC // 4)

            @block.sync
            def _(sp):
                def load_x(c, ch, parts):
                    for part in parts:
                        lo, hi = PARTS[part]
                        wait(sp, xn_ready, (c - 2) * CB + hi)
                        if isinstance(c, int) and c == NCH - 1 and hi == CB:
                            hi = CB - 1
                            sp.dma_start(xs[0:N - r1, ch, hi, :], x[r1:N, :]).then_inc(x_in[ch][part], 16)
                        sp.dma_start(xs[:, ch, lo:hi, :], x[bass.ds((c * CB + lo) * P, (hi - lo) * P), :].rearrange("(u p) d -> p u d", p=P)
                                     ).then_inc(x_in[ch][part], 16)

                def store_nodes(c, ch):
                    sp.wait_ge(qkvs_out, (c + 1) * CB)
                    rows = bass.ds(c * (CB * P), CB * P)
                    sp.dma_start(kv_dram[rows, :].rearrange("(u p) d -> p u d", p=P), nodes[:, ch, :, 0:2 * D]).then_inc(stored[ch], 16)
                    sp.dma_start(skip_dram[rows, :].rearrange("(u p) d -> p u d", p=P), nodes[:, ch, :, 2 * D:3 * D]).then_inc(stored[ch], 16)

                r0, r1 = (NB - CB) * P, (NB - 1) * P
                sp.dma_start(dt_i[:, 0:NC - 1, :], dst[0:FULL * P].rearrange("(c p e) -> p c e", p=P, e=P)).then_inc(d_in, 16)
                sp.wait_ge(pads, 1)
                sp.dma_start(dt_i[0:REST, NC - 1, :], dst[FULL * P:(FULL + REST) * P].rearrange("(p e) -> p e", e=P)).then_inc(d_in, 16)
                sp.dma_start(dt_i[REST:REST + 1, NC - 1, 0:LAST], dst[(FULL + REST) * P:E].rearrange("(p e) -> p e", p=1)).then_inc(d_in, 16)
                load_x(0, 0, range(3))
                for i, w in enumerate((wk, wv, wskip, wq)):
                    sp.dma_start(w4[:, i * D:(i + 1) * D], w).then_inc(w_in, 16)
                for i, b in enumerate((bk, bv, bskip, bq)):
                    sp.dma_start(bias4[:, i * D:(i + 1) * D],
                                 b.rearrange("(a c) -> a c", a=1).broadcast_to([P, D])).then_inc(w_in, 16)
                sp.dma_start(st_i[:, 0:NC - 1, :], src[0:FULL * P].rearrange("(c p e) -> p c e", p=P, e=P)).then_inc(s_in, 16)
                sp.wait_ge(pads, 2)
                sp.dma_start(st_i[0:REST, NC - 1, :], src[FULL * P:(FULL + REST) * P].rearrange("(p e) -> p e", e=P)).then_inc(s_in, 16)
                sp.dma_start(st_i[REST:REST + 1, NC - 1, 0:LAST], src[(FULL + REST) * P:E].rearrange("(p e) -> p e", p=1)).then_inc(s_in, 16)
                sp.wait_ge(d_in, 48)
                sp.dma_start(dst_dram.rearrange("(c p) e -> p c e", p=P), dt_i[:]).then_inc(scratch_out, 16)
                load_x(1, 1, range(3))
                sp.wait_ge(s_in, 48)
                sp.dma_start(src_dram.rearrange("(c p) e -> p c e", p=P), st_i[:]).then_inc(scratch_out, 16)

                def loads_and_store(c, ch):
                    load_x(c + 3, 1 - ch, (0, 1))
                    store_nodes(c, ch)
                    load_x(c + 3, 1 - ch, (2,))

                load_x(2, 0, range(3))
                with sp.Fori(0, PAIRS - 2) as it:
                    for ch in range(2):
                        loads_and_store(2 * it + ch, ch)
                loads_and_store(NCH - 4, 0)
                store_nodes(NCH - 3, 1)
                store_nodes(NCH - 2, 0)
                first = CB // 2
                sp.wait_ge(qkvs_out, NB - CB + first)
                r2 = r0 + first * P
                for table, f0, f1 in ((kv_dram, 0, 2 * D), (skip_dram, 2 * D, 3 * D)):
                    sp.dma_start(table[r0:r2, :].rearrange("(u p) d -> p u d", p=P), nodes[:, 1, 0:first, f0:f1]).then_inc(stored[1], 16)
                sp.wait_ge(qkvs_out, NB)
                for table, f0, f1 in ((kv_dram, 0, 2 * D), (skip_dram, 2 * D, 3 * D)):
                    sp.dma_start(table[r2:r1, :].rearrange("(u p) d -> p u d", p=P), nodes[:, 1, first:CB - 1, f0:f1]).then_inc(stored[1], 16)
                    sp.dma_start(table[r1:N, :], nodes[0:N - r1, 1, CB - 1, f0:f1]).then_inc(stored[1], 16)
                sp.wait_ge(stored[0], 32 * PAIRS)
                sp.wait_ge(stored[1], 32 * (PAIRS - 1) + 96)

            @block.gpsimd
            def _(pool):
                G = nc.gpsimd
                G.memset(dt_i[:, NC - 1, :], PAD).then_inc(pads, 1)
                G.memset(st_i[:, NC - 1, :], 0).then_inc(pads, 1)
                G.memset(ones[:], 1.0).then_inc(consts, 1)
                G.memset(ident[:], 0.0).then_inc(consts, 1)
                pool.wait_ge(consts, 2)
                G.affine_select(out=ident[:], in_=ident[:], compare_op=ALU.not_equal, fill=1.0, base=0,
                                pattern=[[-1, P]], channel_multiplier=1).then_inc(consts, 1)
                G.iota(kint[:], pattern=[[1, NB]], base=0, channel_multiplier=0).then_inc(iotas, 1)
                G.iota(iint[:], pattern=[[P, NC]], base=0, channel_multiplier=1).then_inc(iotas, 1)
                G.memset(cap[:, 0:1], -1.0).then_inc(caps, 1)
                G.memset(cpx[:], -BIG).then_inc(caps, 1)
                pool.wait_ge(ti_ready, 1)
                pool.wait_ge(scratch_out, 32)
                for c in range(NC):
                    at = bass.IndirectOffsetOnAxis(ap=ti[:, c:c + 1], axis=0)
                    G.indirect_dma_start(out=di_i[:, c, :], out_offset=None, in_=dst_dram, in_offset=at).then_inc(di_in, 16)
                for c in range(NC):
                    at = bass.IndirectOffsetOnAxis(ap=ti[:, c:c + 1], axis=0)
                    G.indirect_dma_start(out=si_i[:, c, :], out_offset=None, in_=src_dram, in_offset=at).then_inc(si_in, 16)

                pool.wait_ge(di_in, 16 * NC)
                G.tensor_copy(di, di_i[:]).then_inc(table_chain, 1)
                pool.wait_ge(table_chain, 1)
                G.tensor_tensor(tag, di, btag[:].unsqueeze(2).broadcast_to([P, NC, P]), ALU.add).then_inc(table_chain, 1)
                pool.wait_ge(table_chain, 2)
                pool.wait_ge(caps, 1)
                pool.dma_start(tag_dram[1:1 + NI * P].rearrange("(c p e) -> p c e", p=P, e=P), tag).then_inc(tag_out, 16)
                pool.dma_start(tag_dram[0:1].rearrange("(a e) -> a e", a=1), cap[0:1, 0:1]).then_inc(tag_out, 16)
                pool.dma_start(tag_dram[1 + NI * P:2 + NI * P].rearrange("(a e) -> a e", a=1), cap[0:1, 0:1]).then_inc(tag_out, 16)
                G.tensor_tensor(ndl[:], b128[:].unsqueeze(2).broadcast_to([P, NC, P]), di, ALU.subtract).then_inc(tables_f, 1)
                pool.wait_ge(tag_out, 48)
                pool.dma_start(tagp, tag_dram[0:NI * P].rearrange("(c p e) -> p c e", p=P, e=P)).then_inc(tagp_in, 16)
                pool.dma_start(tagn, tag_dram[2:2 + NI * P].rearrange("(c p e) -> p c e", p=P, e=P)).then_inc(tagp_in, 16)
                pool.wait_ge(si_in, 16 * NC)
                G.tensor_copy(si, si_i[:]).then_inc(tables_f, 1)
                pool.wait_ge(tagp_in, 32)
                G.tensor_tensor(tagp, tag, tagp, ALU.subtract).then_inc(tag_diff, 1)
                G.tensor_tensor(tagn, tag, tagn, ALU.subtract).then_inc(tag_diff, 1)
                pool.wait_ge(pen_ready, 2)
                pool.dma_start(pen_dram[:, 0:P].rearrange("(c p) e -> p c e", p=P), tagp).then_inc(pen_out, 16)
                pool.dma_start(pen_dram[:, P:P + 1].rearrange("(c p) e -> p c e", p=P), tagn[:, :, P - 1:P],
                               allow_slow_non_contiguous=True).then_inc(pen_out, 16)
                pool.wait_ge(tr_sb, 2 * TR)
                pool.dma_start(erec_dram, erec[:].rearrange("e c q f -> e (c q) f")).then_inc(idx_out, 16)
                pool.wait_ge(small_sb, 3)
                pool.dma_start(brow_dram.rearrange("(c i) -> c i", c=NC), bti[:]).then_inc(brow_out, 16)
                for d in range(2):
                    pool.dma_start(cp_dram[:, d, :].rearrange("(c q) f -> c q f", q=4),
                                   cpx[:, d, :, :, :].rearrange("c q h t -> c q (h t)")).then_inc(idx_out, 16)
                pool.wait_ge(brow_out, 16)
                pool.dma_start(brow[:], brow_dram.rearrange("(a i) -> a i", a=1)).then_inc(brow_in, 16)
                pool.wait_ge(idx_out, 48)
                pool.wait_ge(pen_out, 32)
                pool.wait_ge(brow_in, 16)

            @block.vector
            def _(dve):
                V = nc.vector
                done = [0]

                def link(ins):
                    done[0] += 1
                    ins.then_inc(chain, 1)
                    dve.wait_ge(chain, done[0])

                def statistics(turn, m):
                    turn, m = turn + m // (2 * CB), m % (2 * CB)
                    ch, u = m // CB, m % CB
                    for part, (lo, hi) in enumerate(PARTS):
                        if u == lo:
                            last = isinstance(turn, int) and 2 * turn + ch == NCH - 1 and hi == CB
                            dve.wait_ge(x_in[ch][part], 16 * (turn + 1) + (16 if last else 0))
                    V.bn_stats(stats[:, ch, u, :], xs[:, ch, u, :]).then_inc(stats_done, 1)

                def aggregate(turn, m):
                    ch, u = m // CB % 2, m % CB
                    V.bn_aggr(mv[:, ch, u, :], stats[:, ch, u, :]).then_inc(aggr_done, 1)

                V.memset(eps[:], EPS_LN)
                dve.wait_ge(iotas, 2)
                V.tensor_copy(kf[:], kint[:])
                link(V.tensor_copy(ifl[:], iint[:]))
                dve.wait_ge(d_in, 48)
                V.tensor_copy(lastd[:], dt_i[:, :, P - 1])
                link(V.tensor_scalar(k128[:], kf[:], float(P), None, ALU.mult))
                link(V.tensor_tensor(cmp1, lastd[:].unsqueeze(1).broadcast_to([P, NB, NC]),
                                     k128[:].unsqueeze(2).broadcast_to([P, NB, NC]), ALU.is_lt))
                V.tensor_reduce(cnt[:], cmp1, axis=AX.X, op=ALU.add).then_inc(cnt_ready, 1)
                for u in range(CB):
                    statistics(0, u)
                for u in range(CB):
                    dve.wait_ge(stats_done, u + 1)
                    aggregate(0, u)
                dve.wait_ge(count_ps, 1)
                link(V.tensor_tensor(start[:], p_i[:, 0:NB], kf[:], ALU.add))
                V.tensor_tensor(cmp2, start[:].unsqueeze(1).broadcast_to([P, NC, NB]),
                                ifl[:].unsqueeze(2).broadcast_to([P, NC, NB]), ALU.is_le).then_inc(chain, 1)
                done[0] += 1

                def inverse(c, ch):
                    dve.wait_ge(std_done, c + 1)
                    V.reciprocal(rstd[:, ch, :], std[:, ch, :]).then_inc(rstd_done, 1)

                def shifts(c, ch):
                    dve.wait_ge(rstd_done, c + 1)
                    V.scalar_tensor_tensor(shift[:, ch, :], mv[:, ch, :, 0], -1.0, rstd[:, ch, :], ALU.mult, ALU.mult).then_inc(shift_done, 1)

                inverse(0, 0)
                shifts(0, 0)
                dve.wait_ge(chain, done[0])
                link(V.tensor_reduce(bsum[:], cmp2, axis=AX.X, op=ALU.add))
                link(V.tensor_scalar(bf[:], bsum[:], -1.0, None, ALU.add))
                link(V.tensor_tensor(tf[:], ifl[:], bf[:], ALU.subtract))
                V.tensor_scalar(b128[:], bf[:], float(P), None, ALU.mult)
                V.tensor_scalar(btag[:], bf[:], float(PAD + 1), None, ALU.mult)
                V.tensor_copy(ti[:], tf[:]).then_inc(ti_ready, 1)
                for m in range(CB, AHEAD):
                    statistics(0, m)
                for m in range(CB, AHEAD - 1):
                    dve.wait_ge(stats_done, m + 1)
                    aggregate(0, m)
                dve.wait_ge(w_in, 128)

                def step(turn, k):
                    n = 2 * CB * turn + k
                    ch, u = k // CB, k % CB
                    c, nx = 2 * turn + ch, 1 - ch
                    more = not isinstance(c, int) or c + 1 < NCH

                    def exists(block):
                        return not isinstance(block, int) or block < NB

                    if exists(n + AHEAD - 1):
                        wait_apart(dve, w_in, (stats_done, n + AHEAD))
                        aggregate(turn, k + AHEAD - 1)
                    if exists(n + AHEAD):
                        statistics(turn, k + AHEAD)
                    if more and u == 4:
                        inverse(c + 1, nx)
                        shifts(c + 1, nx)
                    if u == 0:
                        wait(dve, stored[ch], 32 * turn)
                    dve.wait_ge(qkvs_ps, n + 1)
                    pq = p_q[k % 2]
                    V.tensor_tensor(nodes[:, ch, u, :], pq[:, 0:3 * D], bias4[:, 0:3 * D], ALU.add)
                    V.tensor_tensor(qt[:, bass.ds(n, 1), :].rearrange("p a d -> p (a d)"), pq[:, 3 * D:NQ], bias4[:, 3 * D:NQ], ALU.add
                                    ).then_inc(qkvs_out, 1)

                def pair(turn):
                    for k in range(2 * CB):
                        step(turn, k)

                pair(0)
                with dve.Fori(1, MID) as turn:
                    pair(turn)
                for i, near in enumerate((tagp, tagn)):
                    dve.wait_ge(tag_diff, i + 1)
                    V.tensor_scalar(near, near, 0.0, -BIG, ALU.not_equal, ALU.mult).then_inc(pen_ready, 1)
                for i, near in enumerate((tagp, tagn)):
                    dve.wait_ge(pen_ready, i + 1)
                    V.tensor_reduce(cp[:, i, :], near, axis=AX.X, op=ALU.add).then_inc(cp_ready, 1)
                dve.wait_ge(small_ps, 1)
                V.tensor_copy(bti[:], p_i[0:NC, 0:P]).then_inc(small_sb, 1)
                dve.wait_ge(caps, 2)
                for d in range(2):
                    dve.wait_ge(small_ps, 2 + d)
                    V.tensor_copy(cpx[:, d, :, :, (1 - d):(1 - d) + BI],
                                  p_i[0:NC, P * (1 + d):P * (2 + d)].rearrange("c (q t) -> c q t", q=4).unsqueeze(2)
                                  .broadcast_to([NC, 4, H, BI])).then_inc(small_sb, 1)
                with dve.Fori(MID, PAIRS - 1) as turn:
                    pair(turn)
                pair(PAIRS - 1)

            @block.scalar
            def _(act):
                S = nc.scalar

                def chunk_std(c, ch):
                    act.wait_ge(aggr_done, (c + 1) * CB)
                    S.activation(std[:, ch, :], mv[:, ch, :, 1], ACT.Sqrt, bias=eps[:, 0:1]).then_inc(std_done, 1)

                def normalise(turn, k):
                    n = 2 * CB * turn + k
                    ch, u = (k // CB) % 2, k % CB
                    if isinstance(n, int) and n >= NB:
                        return
                    if u == 0:
                        act.wait_ge(shift_done, 2 * turn + k // CB + 1)
                    wait(act, xt_ps, n - 1)
                    S.activation(xn[:, k % 2, :], xs[:, ch, u, :], ACT.Identity, scale=rstd[:, ch, u:u + 1],
                                 bias=shift[:, ch, u:u + 1]).then_inc(xn_ready, 1)

                def relu(turn, k):
                    n = 2 * CB * turn + k
                    if isinstance(n, int) and n >= NB:
                        return
                    act.wait_ge(xt_ps, n + 1)
                    wait(act, qkvs_ps, n - 1)
                    S.activation(ht[:, k % 2, :], p_t[k % 2][:, 0:P], ACT.Relu).then_inc(ht_ready, 1)

                def pair(turn):
                    for k in range(2 * CB):
                        normalise(turn, k + 2)
                        relu(turn, k + 1)
                        if k % CB == 3 and not (isinstance(turn, int) and 2 * turn + k // CB + 1 >= NCH):
                            chunk_std(2 * turn + k // CB + 1, 1 - k // CB)

                chunk_std(0, 0)
                normalise(0, 0)
                normalise(0, 1)
                relu(0, 0)
                pair(0)
                with act.Fori(1, MID) as turn:
                    pair(turn)
                for which in range(2):
                    for m in range(TR):
                        w = min(4, NC - 4 * m)
                        act.wait_ge(tr_ps, which * TR + m + 1)
                        pv = p_tr[(which * TR + m) % 2][:, 0:w * P].rearrange("e (c q t) -> e c q t", c=w, q=4)
                        to = erec[:, 4 * m:4 * m + w, :, which * BI:(which + 1) * BI]
                        S.activation(to.bitcast(F32) if which else to, pv, ACT.Copy).then_inc(tr_sb, 1)
                with act.Fori(MID, PAIRS - 1) as turn:
                    pair(turn)
                pair(PAIRS - 1)

            @block.tensor
            def _(pe):
                T = nc.tensor
                pe.wait_ge(consts, 3)
                pe.wait_ge(cnt_ready, 1)
                T.matmul(p_i[:, 0:NB], ones[:], cnt[:], start=True, stop=True).then_inc(count_ps, 1)
                pe.wait_ge(w_in, 128)

                def transpose(turn, k):
                    n = 2 * CB * turn + k
                    if isinstance(n, int) and n >= NB:
                        return
                    pe.wait_ge(xn_ready, n + 1)
                    wait(pe, ht_ready, n - 1)
                    T.transpose(p_t[k % 2][:, 0:P], xn[:, k % 2, :], ident[:]).then_inc(xt_ps, 1)

                def product(turn, k):
                    n = 2 * CB * turn + k
                    pe.wait_ge(ht_ready, n + 1)
                    wait(pe, qkvs_out, n - 1)
                    T.matmul(p_q[k % 2][:], ht[:, k % 2, :], w4[:], start=True, stop=True).then_inc(qkvs_ps, 1)

                def pair(turn):
                    for k in range(2 * CB):
                        transpose(turn, k + 1)
                        product(turn, k)

                transpose(0, 0)
                pair(0)
                with pe.Fori(1, MID) as turn:
                    pair(turn)
                pe.wait_ge(tables_f, 2)
                for which, table in ((0, si), (1, ndl[:])):
                    for m in range(TR):
                        bank = which * TR + m
                        wait(pe, tr_sb, bank - 1)
                        for i in range(min(4, NC - 4 * m)):
                            last = T.transpose(p_tr[bank % 2][:, i * P:(i + 1) * P], table[:, 4 * m + i, :], ident[:])
                        last.then_inc(tr_ps, 1)
                T.transpose(p_i[0:NC, 0:P], bf[:], ident[:]).then_inc(small_ps, 1)
                pe.wait_ge(cp_ready, 2)
                for d in range(2):
                    pe.wait_ge(small_sb, 1 + d)
                    T.transpose(p_i[0:NC, P * (1 + d):P * (2 + d)], cp[:, d, :], ident[:]).then_inc(small_ps, 1)
                with pe.Fori(MID, PAIRS - 1) as turn:
                    pair(turn)
                pair(PAIRS - 1)


def edges(nc, attr, we, dram, qt, acc, ident, brow):
    kv_dram, skip_dram, dst_dram, src_dram, tag_dram, pen_dram, cp_dram, erec_dram, brow_dram, tail_dram = dram
    UNR = 2 * GB
    TURNS = NG // UNR
    PENS = H + 1
    STEPS_LEFT = LAG + 1

    with ExitStack() as ctx:
        def sb(name, shape, dt=F32):
            return ctx.enter_context(nc.sbuf_tensor(name, shape, dt))

        def pb(name, shape):
            return ctx.enter_context(nc.psum_tensor(name, shape, F32))

        def sem(name):
            return ctx.enter_context(nc.semaphore(name))

        val = sb("val", [P, RING, GI, H, CW])
        onehot = sb("onehot", [P, RING, GI, P])
        kvr = sb("kvr", [P, SLOTS, GI, 2 * D])
        araw = sb("araw", [P, SLOTS, GI, A])
        at = sb("at", [P, P])
        st = sb("st", [P, GI, P])
        we4 = sb("we4", [P, GI, D])
        wv = sb("wv", [P, 2, GI, H * CW])
        alpha = sb("alpha", [P, 2, H, BI])
        ex = sb("ex", [P, 2, H, BI])
        erec = sb("erec2", [P, 2, 2 * BI], I32)
        pen = sb("pen", [P, 2, P + 1])
        fwd = sb("fwd", [P, P])
        bwd = sb("bwd", [P, P])
        cin = sb("cin", [P, 2])
        fac = sb("fac", [P, H])
        iota_f = sb("iota_f", [P, P])
        iota_i = fwd[:, :].bitcast(I32)
        sel4 = sb("sel4", [P, H])
        one = sb("one", [1, 1])
        cpr = sb("cpr", [1, 2, 2, H * CW])
        zf = sb("zf", [1, H, CW])
        rf = sb("rf", [1, H, CW])
        zb = sb("zb", [1, H, CW])
        dm = sb("dm", [1, 2, H])

        p_e = pb("p_e", [P, 512])
        p_qd = pb("p_qd", [P, 512])
        p_st = pb("p_st", [P, 512])
        p_ag = [pb(f"p_ag{i}", [P, 512]) for i in range(2)]
        p_at = pb("p_at", [P, 512])
        p_al = pb("p_al", [P, 512])
        p_sm = pb("p_sm", [P, 512])
        p_row, p_col, p_m, p_f = p_sm[0:1, 0:P], p_sm[:, P:P + 1], p_sm[0:1, 132:132 + H], p_sm[:, 140:140 + H]
        p_ex = p_al[:, 256:256 + P]

        kv_in = [sem(f"kv_in{i}") for i in range(SLOTS)]
        attr_in = [sem(f"attr_in{i}") for i in range(SLOTS)]
        erec_in = [sem(f"erec_in{i}") for i in range(2)]
        pen_in = [sem(f"pen_in{i}") for i in range(2)]
        we_in, tail_out, setup, cleared = sem("we_in"), sem("tail_out"), sem("setup"), sem("cleared")
        at_ps, at_sb, st_ps, st_sb, sq_done, onehot_done = (sem(n) for n in ("at_ps", "at_sb", "st_ps", "st_sb", "sq_done", "onehot_done"))
        e_ps, q_ps, k_done, v_done, prod_done, alpha_done = (sem(n) for n in ("e_ps", "q_ps", "k_done", "v_done", "prod_done", "alpha_done"))
        wv_done, wv_last, agg_ps, acc_done, scaled = (sem(n) for n in ("wv_done", "wv_last", "agg_ps", "acc_done", "scaled"))
        al_ps, last_f, row_f, carry_f, z_f, run_f, col_f, cin_f, fwd_done = (
            sem(n) for n in ("al_ps", "last_f", "row_f", "carry_f", "z_f", "run_f", "col_f", "cin_f", "fwd_done"))
        first_b, row_b, z_b, run_b, col_b, cin_b, max_done = (
            sem(n) for n in ("first_b", "row_b", "z_b", "run_b", "col_b", "cin_b", "max_done"))
        diff_done, ext_done, ex_ps, ex_done, m_ps, dm_sub, dm_done, f_ps, f_done = (
            sem(n) for n in ("diff_done", "ext_done", "ex_ps", "ex_done", "m_ps", "dm_sub", "dm_done", "f_ps", "f_done"))
        block = ctx.enter_context(nc.Block())

        def blocks_of(engine, n):
            return nc.values_load_multi_w_load_instructions(
                brow[0:1, bass.ds(GI * n, GI)], engines=[engine], min_val=0, max_val=NB - 1,
                skip_runtime_bounds_check_because="b[i] counts blocks started, out of NB")[1]

        def behind(turn, s):
            j = 2 * turn + s // GB - 1
            return (j, (s // GB + 1) % 2) if not isinstance(j, int) or 0 <= j < NBATCH else (None, None)

        def draining(turn, s):
            return isinstance(turn, int) and turn == TURNS and s >= 0

        def sum_bank(turn, s, i):
            banks = (p_e, p_qd) if draining(turn, s) and s % 2 == 1 else p_ag
            return banks[i // 2][:, (i % 2) * 256:(i % 2) * 256 + H * CW]

        @block.sync
        def _(sp):
            def copy_tail(m):
                rows = E - TAIL0 * P
                to, of, m = ((tail_dram[0:rows, :], attr[TAIL0 * P:E, :], m) if m < GB // 2 else
                             (tail_dram[rows:NTAIL * P, :], attr[0:NTAIL * P - rows, :], m - GB // 2))
                to, of = (t.rearrange("(m a r) f -> m a (r f)", m=GB // 2, r=16)[m] for t in (to, of))
                sp.dma_start(to, of).then_inc(tail_out, 16)

            def load_items(j, jj):
                wait(sp, alpha_done, GB * (j - 1))
                sp.dma_start(erec[:, jj, :], erec_dram[:, bass.ds(j, 1), :].rearrange("e a f -> e (a f)")).then_inc(erec_in[jj], 16)

            def load_pens(j, jj):
                wait(sp, max_done, j - 1)
                wait(sp, run_b, j - 1)
                for h in range(H):
                    sp.dma_start(pen[BI * h:BI * (h + 1), jj, :], pen_dram[bass.ds(j * BI, BI), :]).then_inc(pen_in[jj], 16)
                sp.dma_start(cpr[0:1, jj, :, :].rearrange("a d f -> a (d f)"),
                             cp_dram[bass.ds(j, 1), :, :].rearrange("a d f -> a (d f)")).then_inc(pen_in[jj], 16)

            def step(turn, s, table, tile0):
                n = UNR * turn + s
                jj = s // GB
                j = 2 * turn + jj
                wait(sp, at_ps, n - SLOTS + 1)
                blocks = blocks_of(EngineType.SP, n)
                for i in range(GI):
                    tile = nc.s_assert_within(GI * n + i - blocks[i] - tile0, 0, table.shape[0] // P - 1, skip_runtime_bounds_check_because=(
                        "item i's tile is i - b[i], from 0 to the tile that item i would have with b = 0"))
                    sp.dma_start(araw[:, s % SLOTS, i, :], table[bass.ds(tile * P, P), :]).then_inc(attr_in[s % SLOTS], 16)
                if s % GB == 3:
                    load_pens(j, jj)
                if s % GB == 5 and not (isinstance(j, int) and j + 1 >= NBATCH):
                    load_items(j + 1, 1 - jj)

            load_items(0, 0)
            sp.wait_ge(setup, 1)
            for i in range(GI):
                sp.dma_start(we4[A * i:A * (i + 1), i, :], we).then_inc(we_in, 16)
            for s in range(UNR):
                step(0, s, attr, 0)
                if s >= GB:
                    copy_tail(s - GB)
            whole = (NBATCH - 4) // 2
            with sp.Fori(1, whole) as turn:
                for s in range(UNR):
                    step(turn, s, attr, 0)
            sp.wait_ge(tail_out, 16 * GB)
            for turn in range(whole, TURNS):
                for s in range(UNR):
                    step(turn, s, tail_dram, TAIL0)

        @block.gpsimd
        def _(pool):
            nc.gpsimd.memset(we4[:], 0.0).then_inc(setup, 1)
            nc.gpsimd.iota(iota_i, pattern=[[1, P]], base=0, channel_multiplier=0).then_inc(setup, 1)
            nc.gpsimd.memset(sel4[:], 0.0).then_inc(setup, 1)
            nc.gpsimd.memset(one[:], 1.0).then_inc(setup, 1)
            nc.gpsimd.memset(zb[:], -BIG).then_inc(setup, 1)
            nc.gpsimd.memset(rf[:], -BIG).then_inc(setup, 1)
            pool.wait_ge(setup, 6)
            nc.gpsimd.tensor_copy(iota_f[:], iota_i).then_inc(setup, 1)
            nc.gpsimd.affine_select(out=sel4[:], in_=sel4[:], compare_op=ALU.not_equal, fill=1.0, base=0,
                                    pattern=[[-BI, H]], channel_multiplier=1).then_inc(setup, 1)
            nc.gpsimd.memset(val[:, :, :, :, C:CW], 1.0).then_inc(setup, 1)
            def step(turn, s):
                n = UNR * turn + s
                jj = s // GB
                batch = ((erec_in[jj], 16 * (turn + 1)),) if s % GB == 0 else ()
                wait_apart(pool, setup, (alpha_done, n - SLOTS + 1), *batch)
                for i in range(GI):
                    t = GI * (s % GB) + i
                    nc.gpsimd.indirect_dma_start(
                        out=kvr[:, s % SLOTS, i, :], out_offset=None, in_=kv_dram,
                        in_offset=bass.IndirectOffsetOnAxis(ap=erec[:, jj, t:t + 1], axis=0)).then_inc(kv_in[s % SLOTS], 16)

            for s in range(UNR):
                step(0, s)
            with pool.Fori(1, TURNS) as turn:
                for s in range(UNR):
                    step(turn, s)

        @block.vector
        def _(dve):
            V = nc.vector

            def add_item(turn, s, i, blocks):
                n = UNR * turn + s - LAG - 1
                if not live(n) or i not in range(GI):
                    return
                rows = acc[:, bass.ds(blocks[i], 1), :]
                if i % 2 == 0:
                    dve.wait_ge(agg_ps, 2 * n + i // 2 + 1)
                if i == 0 and starts_batch(s):
                    dve.wait_ge(scaled, 2 * turn + (s - LAG - 1) // GB + 1)
                wait(dve, acc_done, GI * n + i)
                rows = rows.rearrange("p a f -> p (a f)")
                V.tensor_tensor(rows, rows, sum_bank(turn, s - 1, i), ALU.add).then_inc(acc_done, 1)

            def rescale(turn, s, blocks):
                n = UNR * turn + s - LAG - 1
                if not live(n):
                    return
                wait(dve, acc_done, GI * n)
                dve.wait_ge(f_done, 2 * turn + (s - LAG - 1) // GB + 1)
                rows = acc[:, bass.ds(blocks[0], 1), :].rearrange("p a (h c) -> p (a h) c", c=CW)
                V.tensor_tensor(rows, rows, fac[:].unsqueeze(2).broadcast_to([P, H, CW]), ALU.mult).then_inc(scaled, 1)

            def starts_batch(s):
                return (s - LAG - 1) % GB == 0

            def softmax(turn, s, place):
                j, jj = behind(turn, s)
                if j is None:
                    return
                at_ = (s % GB, place)
                al = p_al[:, 0:P]
                if at_ == (0, 0):
                    dve.wait_ge(al_ps, j + 1)
                    wait(dve, ex_ps, j)
                    dve.wait_ge(pen_in[jj], 16 * PENS * (turn + s // GB))
                    V.tensor_tensor_scan(fwd[:], pen[:, jj, 0:P], al, -BIG, ALU.add, ALU.max).then_inc(last_f, 1)
                    V.tensor_copy(zf[:, :, 0], rf[:, :, BI]).then_inc(carry_f, 1)
                elif at_ == (0, 2):
                    dve.wait_ge(carry_f, j + 1)
                    dve.wait_ge(z_f, j + 1)
                    V.tensor_tensor_scan(rf[:].rearrange("a h t -> a (h t)"), cpr[0:1, jj, 0, :],
                                         zf[:].rearrange("a h t -> a (h t)"), -BIG, ALU.add, ALU.max).then_inc(run_f, 1)
                elif at_ == (1, 1):
                    dve.wait_ge(cin_f, j + 1)
                    V.tensor_tensor_scan(fwd[:], pen[:, jj, 0:P], al, cin[:, 0:1], ALU.add, ALU.max).then_inc(fwd_done, 1)
                elif at_ == (1, 2):
                    dve.wait_ge(fwd_done, j + 1)
                    V.tensor_tensor_scan(bwd[:, ::-1], pen[:, jj, P:0:-1], fwd[:, ::-1], -BIG, ALU.add, ALU.max).then_inc(first_b, 1)
                elif at_ == (2, 1):
                    dve.wait_ge(z_b, j + 1)
                    V.tensor_tensor_scan(zb[:].rearrange("a h t -> a (h t)")[:, ::-1], cpr[0:1, jj, 1, ::-1],
                                         zb[:].rearrange("a h t -> a (h t)")[:, ::-1], -BIG, ALU.add, ALU.max).then_inc(run_b, 1)
                elif at_ == (3, 1):
                    dve.wait_ge(cin_b, j + 1)
                    V.tensor_tensor_scan(bwd[:, ::-1], pen[:, jj, P:0:-1], fwd[:, ::-1], cin[:, 1:2], ALU.add, ALU.max).then_inc(max_done, 1)
                elif at_ == (3, 2):
                    dve.wait_ge(max_done, j + 1)
                    V.tensor_tensor(fwd[:], al, bwd[:], ALU.subtract).then_inc(diff_done, 1)
                elif at_ == (4, 0):
                    dve.wait_ge(m_ps, j + 1)
                    V.tensor_tensor(dm[:, 0, :], zf[:, :, 0], p_m, ALU.subtract).then_inc(dm_sub, 1)
                elif at_ == (4, 1):
                    dve.wait_ge(dm_sub, j + 1)
                    V.tensor_scalar(dm[:, 1, :], dm[:, 0, :], 0.0, None, ALU.min).then_inc(dm_done, 1)

            def weigh(turn, s):
                m = UNR * turn + s - LAG
                if not live(m):
                    return
                sm = (s - LAG) % RING
                t0 = GI * ((s - LAG) % GB)
                dve.wait_ge(ex_done, 2 * turn + (s - LAG) // GB + 1)
                wait(dve, agg_ps, 2 * (m - 1))
                dve.wait_ge(v_done, m + 1)
                V.tensor_tensor(wv[:, s % 2, 0:GI - 1, :].rearrange("e i (h c) -> e i h c", h=H), val[:, sm, 0:GI - 1, :, :],
                                ex[:, ((s - LAG) // GB) % 2, :, t0:t0 + GI - 1].rearrange("e h i -> e i h").unsqueeze(3)
                                .broadcast_to([P, GI - 1, H, CW]), ALU.mult).then_inc(wv_done, 1)

            def draining_step(turn, s):
                blocks = blocks_of(EngineType.DVE, UNR * turn + s - LAG - 1)
                weigh(turn, s)
                if starts_batch(s):
                    rescale(turn, s, blocks)
                for i in range(GI):
                    add_item(turn, s, i, blocks)
                    if i < 3:
                        softmax(turn, s, i)

            def step(turn, s):
                n = UNR * turn + s
                jj = s // GB
                j = 2 * turn + jj
                slot = s % SLOTS
                here = live(n)
                kpart = kvr[:, slot, :, 0:D]
                blocks = blocks_of(EngineType.DVE, n - LAG - 1) if live(n - LAG - 1) else None
                if here:
                    dve.wait_ge(kv_in[slot], 16 * GI * (UNR // SLOTS * turn + s // SLOTS + 1))
                    dve.wait_ge(e_ps, n + 1)
                    pe_ = p_e[:].rearrange("e (i c) -> e i c", i=GI)
                    V.tensor_tensor(kpart, kpart, pe_, ALU.add).then_inc(k_done, 1)
                late = 1 if starts_batch(s) else 0
                add_item(turn, s, 0 - late, blocks)
                if here:
                    V.tensor_tensor(val[:, s % RING, :, :, 0:C], kvr[:, slot, :, D:2 * D].rearrange("e i (h c) -> e i h c", h=H),
                                    p_e[:].rearrange("e (i h c) -> e i h c", i=GI, h=H), ALU.add).then_inc(v_done, 1)
                if late:
                    rescale(turn, s, blocks)
                add_item(turn, s, 1 - 2 * late, blocks)
                softmax(turn, s, 0)
                if here:
                    dve.wait_ge(q_ps, n + 1)
                    dve.wait_ge(k_done, n + 1)
                    V.tensor_tensor(kpart, kpart, p_qd[:].rearrange("e (i c) -> e i c", i=GI), ALU.mult).then_inc(prod_done, 1)
                add_item(turn, s, 2 - 2 * late, blocks)
                weigh(turn, s)
                if late:
                    add_item(turn, s, 1, blocks)
                softmax(turn, s, 1)
                add_item(turn, s, 3 - late, blocks)
                if here:
                    dve.wait_ge(prod_done, n + 1)
                    if s % GB == 0:
                        wait(dve, al_ps, j - 1)
                    t0 = GI * (s % GB)
                    V.tensor_reduce(alpha[:, jj, :, t0:t0 + GI].rearrange("e h i -> e i h"),
                                    kpart.rearrange("e i (h c) -> e i h c", h=H), axis=AX.X, op=ALU.add).then_inc(alpha_done, 1)
                if late:
                    add_item(turn, s, 3, blocks)
                softmax(turn, s, 2)

            dve.wait_ge(setup, 9)
            part = -(-NB // (LAG - 1))
            for s in range(UNR):
                if 1 <= s < LAG:
                    V.memset(acc[:, (s - 1) * part:min(NB, s * part), :], 0.0).then_inc(cleared, 1)
                elif s == LAG + 1:
                    dve.wait_ge(cleared, LAG - 1)
                step(0, s)
            with dve.Fori(1, TURNS) as turn:
                for s in range(UNR):
                    step(turn, s)
            for s in range(STEPS_LEFT):
                (step if s == GB // 2 else draining_step)(TURNS, s)

        @block.scalar
        def _(act):
            S = nc.scalar

            def one_hots(turn, s):
                n = UNR * turn + s
                if not live(n):
                    return
                jj = (s // GB) % 2
                slot = s % RING
                act.wait_ge(erec_in[jj], 16 * (turn + s // UNR + 1))
                wait(act, agg_ps, 2 * (n - RING + 1))
                for i in range(GI):
                    t = BI + GI * (s % GB) + i
                    last = S.activation(onehot[:, slot, i, :], iota_f[:], ACT.Square, bias=erec[:, jj, t:t + 1].bitcast(F32))
                last.then_inc(sq_done, 1)
                act.wait_ge(sq_done, n + 1)
                S.activation(onehot[:, slot, :, :], onehot[:, slot, :, :], ACT.Relu, scale=-1.0, bias=1.0).then_inc(onehot_done, 1)

            def copies(turn, s):
                n = UNR * turn + s
                if not live(n):
                    return
                act.wait_ge(at_ps, n + 1)
                wait(act, e_ps, n)
                S.activation(at[:], p_at[:, 0:P], ACT.Copy).then_inc(at_sb, 1)
                act.wait_ge(st_ps, n + 1)
                wait(act, q_ps, n)
                S.activation(st[:].rearrange("p i e -> p (i e)"), p_st[:], ACT.Copy).then_inc(st_sb, 1)

            row = p_row.rearrange("a (h t) -> a h t", h=H)

            def weigh_last(turn, s):
                m = UNR * turn + s - LAG
                if not live(m):
                    return
                t = GI * ((s - LAG) % GB) + GI - 1
                act.wait_ge(ex_done, 2 * turn + (s - LAG) // GB + 1)
                wait(act, agg_ps, 2 * (m - 1))
                act.wait_ge(v_done, m + 1)
                for h in range(H):
                    last = S.activation(wv[:, s % 2, GI - 1, h * CW:(h + 1) * CW], val[:, (s - LAG) % RING, GI - 1, h, :], ACT.Copy,
                                        scale=ex[:, ((s - LAG) // GB) % 2, h, t:t + 1])
                last.then_inc(wv_last, 1)

            def carries(s, j):
                if s == 1:
                    act.wait_ge(col_f, j + 1)
                    S.activation(cin[:, 0:1], p_col, ACT.Copy).then_inc(cin_f, 1)
                elif s == 2:
                    act.wait_ge(row_b, j + 1)
                    S.activation(zb[:, :, 0:BI], row, ACT.Copy).then_inc(z_b, 1)
                elif s == 3:
                    act.wait_ge(col_b, j + 1)
                    S.activation(cin[:, 1:2], p_col, ACT.Copy).then_inc(cin_b, 1)

            def step(turn, s):
                j, jj = behind(turn, s)
                if s % GB == 4 and j is not None:
                    act.wait_ge(diff_done, j + 1)
                    S.activation(fwd[:], fwd[:], ACT.Exp, scale=SCALE).then_inc(ext_done, 1)
                    act.wait_ge(ex_ps, j + 1)
                    wait(act, wv_done, GB * (j - 1))
                    S.activation(ex[:, jj, :, :].rearrange("e h t -> e (h t)"), p_ex, ACT.Copy).then_inc(ex_done, 1)
                copies(turn, s + 1)
                if j is not None:
                    carries(s % GB, j)
                weigh_last(turn, s)
                if j is not None and s % GB == 0:
                    act.wait_ge(row_f, j + 1)
                    S.activation(zf[:, :, 1:CW], row, ACT.Copy).then_inc(z_f, 1)
                one_hots(turn, s + 2)
                if s % GB == 4 and j is not None:
                    act.wait_ge(f_ps, j + 1)
                    wait(act, scaled, j)
                    S.activation(fac[:], p_f, ACT.Exp, scale=SCALE).then_inc(f_done, 1)

            act.wait_ge(setup, 7)
            one_hots(0, 0)
            copies(0, 0)
            one_hots(0, 1)
            for s in range(UNR):
                step(0, s)
            with act.Fori(1, TURNS - 1) as turn:
                for s in range(UNR):
                    step(turn, s)
            for s in range(UNR):
                step(TURNS - 1, s)
            for s in range(STEPS_LEFT):
                step(TURNS, s)

        @block.tensor
        def _(pe):
            T = nc.tensor

            def transposes(turn, s):
                n = UNR * turn + s
                if not live(n):
                    return
                slot = s % SLOTS
                pe.wait_ge(attr_in[slot], 16 * GI * (UNR // SLOTS * turn + s // SLOTS + 1))
                wait(pe, at_sb, n)
                T.transpose(p_at[:, 0:P], araw[:, slot, :, :].rearrange("e i a -> e (i a)"), ident[:]).then_inc(at_ps, 1)
                pe.wait_ge(onehot_done, n + 1)
                wait(pe, st_sb, n)
                for i in range(GI):
                    last = T.transpose(p_st[:, i * P:(i + 1) * P], onehot[:, s % RING, i, :], ident[:])
                last.then_inc(st_ps, 1)

            def edge_terms(turn, s):
                n = UNR * turn + s
                if not live(n):
                    return
                pe.wait_ge(at_sb, n + 1)
                wait(pe, v_done, n)
                T.matmul(p_e[:], at[:], we4[:].rearrange("a i c -> a (i c)"), start=True, stop=True).then_inc(e_ps, 1)

            def queries(turn, s):
                n = UNR * turn + s
                if not live(n):
                    return
                blocks = blocks_of(EngineType.PE, n)
                pe.wait_ge(st_sb, n + 1)
                wait(pe, prod_done, n)
                for i in range(GI):
                    last = T.matmul(p_qd[:, i * P:(i + 1) * P], st[:, i, :], qt[:, bass.ds(blocks[i], 1), :].rearrange("p a d -> p (a d)"),
                                    start=True, stop=True)
                last.then_inc(q_ps, 1)

            def sums(turn, s):
                n = UNR * turn + s
                if not live(n):
                    return
                pe.wait_ge(wv_done, n + 1)
                if draining(turn, s + LAG) and s + LAG == 1:
                    pe.wait_ge(v_done, NG)
                    pe.wait_ge(prod_done, NG)
                for i in range(GI):
                    if i % 2 == 0 and draining(turn, s + LAG - 1):
                        if s + LAG >= 2:
                            pe.wait_ge(acc_done, GI * (n - 2) + i + 2)
                    elif i % 2 == 0:
                        wait(pe, acc_done, GI * (n - 1) + i + 2)
                    if i == GI - 1:
                        pe.wait_ge(wv_last, n + 1)
                    last = T.matmul(sum_bank(turn, s + LAG, i), onehot[:, s % RING, i, :],
                                    wv[:, s % 2, i, :], start=True, stop=True)
                    if i % 2 == 1:
                        last.then_inc(agg_ps, 1)

            def softmax(turn, s, place):
                j, jj = behind(turn, s)
                if j is None:
                    return
                at_ = (s % GB, place)
                if at_ == (0, 0):
                    pe.wait_ge(alpha_done, GB * (j + 1))
                    wait(pe, ex_done, j)
                    T.transpose(p_al[:, 0:P], alpha[:, jj, :, :].rearrange("e h t -> e (h t)"), ident[:]).then_inc(al_ps, 1)
                elif at_ == (0, 1):
                    pe.wait_ge(last_f, j + 1)
                    wait(pe, f_done, j)
                    T.matmul(p_row, fwd[:, P - 1:P], ident[:], start=True, stop=True).then_inc(row_f, 1)
                elif at_ == (1, 0):
                    wait_apart(pe, setup, (run_f, j + 1))
                    for h in range(H):
                        last = T.matmul(p_col[BI * h:BI * (h + 1), :], rf[0:1, h, 0:BI], one[:], start=True, stop=True)
                    last.then_inc(col_f, 1)
                elif at_ == (2, 0):
                    pe.wait_ge(first_b, j + 1)
                    T.matmul(p_row, bwd[:, 0:1], ident[:], start=True, stop=True).then_inc(row_b, 1)
                elif at_ == (3, 0):
                    wait_apart(pe, setup, (run_b, j + 1))
                    for h in range(H):
                        last = T.matmul(p_col[BI * h:BI * (h + 1), :], zb[0:1, h, 1:CW], one[:], start=True, stop=True)
                    last.then_inc(col_b, 1)
                elif at_ == (4, 0):
                    pe.wait_ge(max_done, j + 1)
                    T.matmul(p_m, bwd[:, 0:1], sel4[:], start=True, stop=True).then_inc(m_ps, 1)
                    pe.wait_ge(ext_done, j + 1)
                    T.transpose(p_ex, fwd[:], ident[:]).then_inc(ex_ps, 1)
                elif at_ == (4, 2):
                    pe.wait_ge(dm_done, j + 1)
                    T.matmul(p_f, onehot[0:1, jj * GB, 0, :], dm[:, 1, :], start=True, stop=True).then_inc(f_ps, 1)

            def step(turn, s):
                softmax(turn, s, 0)
                transposes(turn, s + 1)
                edge_terms(turn, s + 1)
                if draining(turn, s) and s not in (0, GB // 2):
                    sums(turn, s - LAG)
                    softmax(turn, s, 1)
                else:
                    softmax(turn, s, 1)
                    queries(turn, s + 1)
                    sums(turn, s - LAG)
                softmax(turn, s, 2)

            pe.wait_ge(setup, 8)
            pe.wait_ge(we_in, 16 * GI)
            transposes(0, 0)
            edge_terms(0, 0)
            queries(0, 0)
            for s in range(UNR):
                step(0, s)
            with pe.Fori(1, TURNS - 1) as turn:
                for s in range(UNR):
                    step(turn, s)
            for s in range(UNR):
                step(TURNS - 1, s)
            for s in range(STEPS_LEFT):
                step(TURNS, s)


def output(nc, x, w1, b1, w2, b2, out, dram, acc, ident):
    skip_dram = dram[1]
    WID = 4
    WHOLE = NB // WID
    REST = NB - WHOLE * WID
    BUFS = 4
    TURNS = WHOLE // BUFS

    with ExitStack() as ctx:
        def sb(name, shape, dt=F32):
            return ctx.enter_context(nc.sbuf_tensor(name, shape, dt))

        def sem(name):
            return ctx.enter_context(nc.semaphore(name))

        xs = sb("x3", [P, BUFS, WID, D])
        sk = sb("skip3", [P, BUFS, WID, D])
        w1s, w2s = sb("w1s", [P, D]), sb("w2s", [P, D])
        b1s, b2s = sb("b1s", [P, 1]), sb("b2s", [P, 1])
        den = sb("den", [P, NB, H])
        o = sb("o", [P, BUFS, WID, D])
        ot = sb("ot", [P, WID * P])
        h1 = sb("h1", [P, WID * P])
        h2 = sb("h2", [P, WID * P])
        res = sb("res", [P, BUFS, WID, D])
        p_o, p_1, p_2, p_3 = (ctx.enter_context(nc.psum_tensor(f"p3_{i}", [P, 512], F32)) for i in range(4))
        x_loaded = [sem(f"x_loaded{i}") for i in range(BUFS)]
        skip_loaded = [sem(f"skip_loaded{i}") for i in range(BUFS)]
        w_in3 = sem("w_in3")
        den_add, den_inv, normed, out_ready, xo_ready = (sem(n) for n in ("den_add", "den_inv", "normed", "out_ready", "xo_ready"))
        ot_ps, ot_sb, h1_ps, h1_sb, h2_ps, h2_sb, y_ps, res_ready = (
            sem(n) for n in ("ot_ps", "ot_sb", "h1_ps", "h1_sb", "h2_ps", "h2_sb", "y_ps", "res_ready"))
        out_stored = [sem(f"out_stored{i}") for i in range(BUFS)]
        block = ctx.enter_context(nc.Block())

        def whole(g):
            return not isinstance(g, int) or 0 <= g < WHOLE

        def width(g):
            return WID if whole(g) else REST if g == WHOLE else 0

        def each_step(engine, step, left):
            for s in range(BUFS):
                step(0, s)
            with engine.Fori(1, TURNS - 1) as turn:
                for s in range(BUFS):
                    step(turn, s)
            for turn in range(TURNS - 1, TURNS + 1):
                for s in range(BUFS if turn < TURNS else left):
                    step(turn, s)

        r0, r1 = WHOLE * WID * P, (NB - 1) * P

        def load(sp, g, k, buffer, table, loaded):
            if whole(g):
                rows = bass.ds(g * (WID * P), WID * P)
                sp.dma_start(buffer[:, k, :, :], table[rows, :].rearrange("(u p) d -> p u d", p=P)).then_inc(loaded, 16)
            elif width(g):
                sp.dma_start(buffer[:, k, 0:REST - 1, :], table[r0:r1, :].rearrange("(u p) d -> p u d", p=P)).then_inc(loaded, 16)
                sp.dma_start(buffer[0:N - r1, k, REST - 1, :], table[r1:N, :]).then_inc(loaded, 16)

        @block.sync
        def _(sp):
            for k in range(BUFS):
                load(sp, k, k, sk, skip_dram, skip_loaded[k])
                load(sp, k, k, xs, x, x_loaded[k])
                if k == 0:
                    sp.dma_start(w1s[:], w1).then_inc(w_in3, 16)
                    sp.dma_start(w2s[:], w2).then_inc(w_in3, 16)
                    sp.dma_start(b1s[:], b1.rearrange("(c a) -> c a", a=1)).then_inc(w_in3, 16)
                    sp.dma_start(b2s[:], b2.rearrange("(c a) -> c a", a=1)).then_inc(w_in3, 16)

            def step(turn, s):
                g = BUFS * turn + s
                if width(g + BUFS):
                    sp.wait_ge(out_ready, g + 1)
                    load(sp, g + BUFS, s, sk, skip_dram, skip_loaded[s])
                    sp.wait_ge(xo_ready, g + 1)
                    load(sp, g + BUFS, s, xs, x, x_loaded[s])
                sp.wait_ge(res_ready, g + 1)
                if whole(g):
                    sp.dma_start(out[bass.ds(g * (WID * P), WID * P), :].rearrange("(u p) d -> p u d", p=P), res[:, s, :, :]
                                 ).then_inc(out_stored[s], 16)
                else:
                    sp.dma_start(out[r0:r1, :].rearrange("(u p) d -> p u d", p=P), res[:, s, 0:REST - 1, :]).then_inc(out_stored[s], 16)
                    sp.dma_start(out[r1:N, :], res[0:N - r1, s, REST - 1, :]).then_inc(out_stored[s], 16)

            each_step(sp, step, 1)
            for k in range(BUFS):
                sp.wait_ge(out_stored[k], 16 * TURNS + (32 if k == WHOLE % BUFS else 0))

        @block.gpsimd
        def _(pool):
            def step(turn, s):
                g = BUFS * turn + s
                w = width(g)
                pool.wait_ge(out_ready, g + 1)
                pool.wait_ge(x_loaded[s], 16 * (turn + 1) + 16 * (w < WID))
                wait(pool, out_stored[s], 16 * turn)
                nc.gpsimd.tensor_tensor(res[:, s, 0:w, :], o[:, s, 0:w, :], xs[:, s, 0:w, :], ALU.add).then_inc(xo_ready, 1)

            each_step(pool, step, 1)

        @block.vector
        def _(dve):
            V = nc.vector
            sums = acc[:].rearrange("p b (h c) -> p b h c", c=CW)
            V.tensor_scalar(den[:], sums[:, :, :, C], EPS_SUM, None, ALU.add).then_inc(den_add, 1)
            dve.wait_ge(den_add, 1)
            V.reciprocal(den[:], den[:]).then_inc(den_inv, 1)
            dve.wait_ge(den_inv, 1)

            def step(turn, s):
                g = BUFS * turn + s
                w = width(g)
                if w:
                    rows = acc[:, bass.ds(g * WID, w), :].rearrange("p u (h c) -> p u h c", c=CW)
                    wait(dve, ot_ps, g - BUFS + 1)
                    wait(dve, xo_ready, g - BUFS + 1)
                    V.tensor_tensor(o[:, s, 0:w, :].rearrange("p u (h c) -> p u h c", h=H), rows[:, :, :, 0:C],
                                    den[:, bass.ds(g * WID, w), :].unsqueeze(3).broadcast_to([P, w, H, C]), ALU.mult).then_inc(normed, 1)
                v, k = width(g - 3), (s - 3) % BUFS
                if v:
                    dve.wait_ge(y_ps, g - 2)
                    dve.wait_ge(xo_ready, g - 2)
                    V.tensor_tensor(res[:, k, 0:v, :].rearrange("p u d -> p (u d)"), res[:, k, 0:v, :].rearrange("p u d -> p (u d)"),
                                    p_3[:, 0:v * D], ALU.add).then_inc(res_ready, 1)
                if w:
                    dve.wait_ge(normed, g + 1)
                    dve.wait_ge(skip_loaded[s], 16 * (turn + 1) + 16 * (w < WID))
                    V.tensor_tensor(o[:, s, 0:w, :], o[:, s, 0:w, :], sk[:, s, 0:w, :], ALU.add).then_inc(out_ready, 1)

            each_step(dve, step, 4)

        @block.scalar
        def _(act):
            S = nc.scalar

            def transposed(g):
                m = width(g) * P
                if m:
                    act.wait_ge(ot_ps, g + 1)
                    wait(act, h1_ps, g)
                    S.activation(ot[:, 0:m], p_o[:, 0:m], ACT.Copy).then_inc(ot_sb, 1)

            def step(turn, s):
                g = BUFS * turn + s
                m = width(g) * P
                act.wait_ge(h1_ps, g + 1)
                S.activation(h1[:, 0:m], p_1[:, 0:m], ACT.Gelu_apprx_tanh, bias=b1s[:, 0:1]).then_inc(h1_sb, 1)
                transposed(g + 1)
                act.wait_ge(h2_ps, g + 1)
                wait(act, y_ps, g)
                S.activation(h2[:, 0:m], p_2[:, 0:m], ACT.Gelu_apprx_tanh, bias=b2s[:, 0:1]).then_inc(h2_sb, 1)

            act.wait_ge(w_in3, 64)
            transposed(0)
            each_step(act, step, 1)

        @block.tensor
        def _(pe):
            T = nc.tensor

            def transposes_in(g, k):
                if width(g):
                    pe.wait_ge(out_ready, g + 1)
                    wait(pe, ot_sb, g)
                    for u in range(width(g)):
                        last = T.transpose(p_o[:, u * P:(u + 1) * P], o[:, k, u, :], ident[:])
                    last.then_inc(ot_ps, 1)

            def transposes_out(g):
                if width(g):
                    pe.wait_ge(h2_sb, g + 1)
                    wait(pe, res_ready, g)
                    for u in range(width(g)):
                        last = T.transpose(p_3[:, u * P:(u + 1) * P], h2[:, u * P:(u + 1) * P], ident[:])
                    last.then_inc(y_ps, 1)

            def step(turn, s):
                g = BUFS * turn + s
                m = width(g) * P
                if m:
                    pe.wait_ge(ot_sb, g + 1)
                    wait(pe, h1_sb, g)
                    T.matmul(p_1[:, 0:m], w1s[:], ot[:, 0:m], start=True, stop=True).then_inc(h1_ps, 1)
                transposes_out(g - 1)
                transposes_in(g + 1, (s + 1) % BUFS)
                if m:
                    pe.wait_ge(h1_sb, g + 1)
                    wait(pe, h2_sb, g)
                    T.matmul(p_2[:, 0:m], w2s[:], h1[:, 0:m], start=True, stop=True).then_inc(h2_ps, 1)

            pe.wait_ge(w_in3, 64)
            transposes_in(0, 0)
            each_step(pe, step, 2)


def graph_transformer(nc, x, src, dst, attr, wq, bq, wk, bk, wv, bv, we, wskip, bskip, w1, b1, w2, b2, out):
    def scratch(name, shape, dt=F32):
        return nc.dram_tensor(name, shape, dt, kind="Internal").ap()

    dram = (scratch("kv_rows", (N, 2 * D)), scratch("skip_rows", (N, D)),
            scratch("dst_tiles", (NI, P), I32), scratch("src_tiles", (NI, P), I32),
            scratch("tags", (NI * P + 2,)), scratch("penalties", (NI, P + 1)),
            scratch("carry_penalties", (NBATCH, 2, H * CW)), scratch("item_edges", (P, NBATCH, 2 * BI), I32),
            scratch("item_blocks", (NI,), I32), scratch("attr_end", (NTAIL * P, A)))
    with ExitStack() as ctx:
        acc = ctx.enter_context(nc.sbuf_tensor("acc", [P, NB, H * CW], F32))
        ident = ctx.enter_context(nc.sbuf_tensor("ident", [P, P], F32))
        with ExitStack() as inner:
            qt = inner.enter_context(nc.sbuf_tensor("qt", [P, NB, D], F32))
            brow = inner.enter_context(nc.sbuf_tensor("brow", [1, NI], I32))
            index_and_nodes(nc, x, src, dst, attr, wq, bq, wk, bk, wv, bv, wskip, bskip, dram, qt, acc, ident, brow)
            edges(nc, attr, we, dram, qt, acc, ident, brow)
        output(nc, x, w1, b1, w2, b2, out, dram, acc, ident)


_INS = ['x', 'src', 'dst', 'edge_attr_32', 'L0_gnn_Wq', 'L0_gnn_bq', 'L0_gnn_Wk', 'L0_gnn_bk', 'L0_gnn_Wv', 'L0_gnn_bv',
        'L0_gnn_We', 'L0_gnn_Wskip', 'L0_gnn_bskip', 'L0_gnn_W1', 'L0_gnn_b1', 'L0_gnn_W2', 'L0_gnn_b2']
_OUTS = [((12500, 128), 'float32')]


def kernel(**inputs):
    import numpy as _np
    import concourse.bacc as _bacc
    from concourse import mybir as _mybir
    from concourse.bass_utils import run_bass_kernel_spmd as _run

    nc = _bacc.Bacc("TRN2", target_bir_lowering=False, num_devices=1)
    arrays, args = {}, []
    for name in _INS:
        a = _np.ascontiguousarray(inputs[name])
        arrays[f"in_{name}_dram"] = a
        args.append(nc.dram_tensor(f"in_{name}_dram", a.shape, _mybir.dt.from_np(a.dtype), kind="ExternalInput").ap())
    for i, (shape, dtype) in enumerate(_OUTS):
        dt = _mybir.dt.from_np(_np.dtype(dtype))
        args.append(nc.dram_tensor(f"out_{i}_dram", shape, dt, kind="ExternalOutput").ap())
    graph_transformer(nc, *args)
    r = _run(nc, [arrays], core_ids=[0])
    got = tuple(r.results[0][f"out_{i}_dram"] for i in range(len(_OUTS)))
    return got[0]
```
